# Optimizing a Trainium2 kernel written in Bass

```python
import numpy as np
import jax
import jax.numpy as jnp

def _softmax(x, axis=-1):
    return jax.nn.softmax(x, axis=axis)

def _gelu(x):
    return jax.nn.gelu(x, approximate=True)

def _silu(x):
    return jax.nn.silu(x)

def _sigmoid(x):
    return jax.nn.sigmoid(x)

def _layernorm(x, axis=-1, eps=1e-05):
    m = jnp.mean(x, axis=axis, keepdims=True)
    v = jnp.var(x, axis=axis, keepdims=True)
    return (x - m) / jnp.sqrt(v + eps)

def _scatter_add(tgt, idx, src, axis=0):
    return tgt.at[idx].add(src)

def _segment_sum(src, seg, n):
    return jax.ops.segment_sum(src, seg, n)
kernel_name = 'mk_adaln_d1_jaxref_r8_0c657d'

def setup_inputs(seed: int=0):
    np.random.seed(seed)
    _w = jnp.asarray

    def _L0_attn_setup():
        import jax, jax.numpy as jnp
        import numpy as np
        from jax import lax
        B, L, D_MODEL = (2, 256, 128)
        D_INNER, D_STATE, DT_RANK, D_CONV = (256, 16, 64, 4)

        def _silu(v):
            return v * jax.nn.sigmoid(v)

        def _mamba_forward(x, in_proj_w, conv_w, conv_b, x_proj_w, dt_proj_w, dt_proj_b, A_log, D, out_proj_w):
            b, l, _ = x.shape
            xr = jnp.einsum('bld,ed->ble', x, in_proj_w)
            xs, res = jnp.split(xr, 2, axis=-1)
            xc = jnp.transpose(xs, (0, 2, 1))
            xc = lax.conv_general_dilated(xc, conv_w, window_strides=(1,), padding=[(D_CONV - 1, 0)], feature_group_count=D_INNER, dimension_numbers=('NCH', 'OIH', 'NCH')) + conv_b[None, :, None]
            u = _silu(jnp.transpose(xc, (0, 2, 1)))
            A = -jnp.exp(A_log)
            x_dbl = jnp.einsum('bld,ed->ble', u, x_proj_w)
            dt, Bm, Cm = jnp.split(x_dbl, [DT_RANK, DT_RANK + D_STATE], axis=-1)
            delta = jax.nn.softplus(jnp.einsum('blr,dr->bld', dt, dt_proj_w) + dt_proj_b)
            deltaA = jnp.exp(jnp.einsum('bld,dn->bldn', delta, A))
            deltaBu = jnp.einsum('bld,bln,bld->bldn', delta, Bm, u)

            def step(h, inp):
                dA, dBu, c = inp
                h = dA * h + dBu
                y = jnp.einsum('bdn,bn->bd', h, c)
                return (h, y)
            xs_scan = (jnp.transpose(deltaA, (1, 0, 2, 3)), jnp.transpose(deltaBu, (1, 0, 2, 3)), jnp.transpose(Cm, (1, 0, 2)))
            h0 = jnp.zeros((b, D_INNER, D_STATE), u.dtype)
            _, ys = lax.scan(step, h0, xs_scan)
            y = jnp.transpose(ys, (1, 0, 2)) + u * D
            y = y * _silu(res)
            return jnp.einsum('bld,ed->ble', y, out_proj_w)
        key = jax.random.key(seed)
        ks = jax.random.split(key, 10)
        s = 0.02
        A_log = jnp.log(jnp.broadcast_to(jnp.arange(1, D_STATE + 1, dtype=jnp.float32), (D_INNER, D_STATE)))
        return {'x': jax.random.normal(ks[0], (B, L, D_MODEL), jnp.float32), 'in_proj_w': jax.random.normal(ks[1], (2 * D_INNER, D_MODEL), jnp.float32) * s, 'conv_w': jax.random.normal(ks[2], (D_INNER, 1, D_CONV), jnp.float32) * s, 'conv_b': jax.random.normal(ks[3], (D_INNER,), jnp.float32) * s, 'x_proj_w': jax.random.normal(ks[4], (DT_RANK + 2 * D_STATE, D_INNER), jnp.float32) * s, 'dt_proj_w': jax.random.normal(ks[5], (D_INNER, DT_RANK), jnp.float32) * s, 'dt_proj_b': jax.random.normal(ks[6], (D_INNER,), jnp.float32) * s, 'A_log': A_log, 'D': jnp.ones((D_INNER,), jnp.float32), 'out_proj_w': jax.random.normal(ks[7], (D_MODEL, D_INNER), jnp.float32) * s}
    _L0_attn_in = _L0_attn_setup()

    def _L0_ffn_setup():
        import jax, jax.numpy as jnp
        import numpy as np
        B, S, D = (1, 256, 128)
        E, F = (16, 128)
        NG, TKG, K = (4, 2, 4)
        NSH = 2
        SCALE = 2.5
        STD = 0.02
        EPG = E // NG

        def _route(x_flat, router_w, bias):
            logits = x_flat.astype(jnp.float32) @ router_w.T
            scores = jax.nn.sigmoid(logits)
            s = scores + bias[None, :]
            sg = s.reshape(-1, NG, EPG)
            group_score = jax.lax.top_k(sg, 2)[0].sum(-1)
            gidx = jax.lax.top_k(group_score, TKG)[1]
            gmask = jnp.sum(jax.nn.one_hot(gidx, NG, dtype=jnp.float32), axis=1) > 0
            emask = jnp.repeat(gmask, EPG, axis=1)
            masked = jnp.where(emask, s, -1.0)
            topk_idx = jax.lax.top_k(masked, K)[1]
            tw = jnp.take_along_axis(scores, topk_idx, axis=1)
            tw = tw / (tw.sum(-1, keepdims=True) + 1e-20)
            tw = tw * SCALE
            return (topk_idx, tw)
        key = jax.random.key(seed)
        ks = jax.random.split(key, 8)
        return {'hidden_states': jax.random.normal(ks[0], (B, S, D), jnp.float32), 'router_w': jax.random.normal(ks[1], (E, D), jnp.float32) * STD, 'bias': jnp.zeros((E,), jnp.float32), 'gate_w': jax.random.normal(ks[2], (E, D, F), jnp.float32) * STD, 'up_w': jax.random.normal(ks[3], (E, D, F), jnp.float32) * STD, 'down_w': jax.random.normal(ks[4], (E, F, D), jnp.float32) * STD, 'sh_gate_w': jax.random.normal(ks[5], (D, NSH * F), jnp.float32) * STD, 'sh_up_w': jax.random.normal(ks[6], (D, NSH * F), jnp.float32) * STD, 'sh_down_w': jax.random.normal(ks[7], (NSH * F, D), jnp.float32) * STD}
    _L0_ffn_in = _L0_ffn_setup()
    _L0_c = _w((lambda *s: np.random.randn(*s).astype(np.float32) * 0.05)(1, 128))
    _L0_wmod = _w((lambda *s: np.random.randn(*s).astype(np.float32) * 0.05)(128, 6 * 128) * 128 ** (-0.5))
    _d = {'L0_attn_x': _L0_attn_in['x'], 'L0_attn_in_proj_w': _L0_attn_in['in_proj_w'], 'L0_attn_conv_w': _L0_attn_in['conv_w'], 'L0_attn_conv_b': _L0_attn_in['conv_b'], 'L0_attn_x_proj_w': _L0_attn_in['x_proj_w'], 'L0_attn_dt_proj_w': _L0_attn_in['dt_proj_w'], 'L0_attn_dt_proj_b': _L0_attn_in['dt_proj_b'], 'L0_attn_A_log': _L0_attn_in['A_log'], 'L0_attn_D': _L0_attn_in['D'], 'L0_attn_out_proj_w': _L0_attn_in['out_proj_w'], 'L0_ffn_router_w': _L0_ffn_in['router_w'], 'L0_ffn_bias': _L0_ffn_in['bias'], 'L0_ffn_gate_w': _L0_ffn_in['gate_w'], 'L0_ffn_up_w': _L0_ffn_in['up_w'], 'L0_ffn_down_w': _L0_ffn_in['down_w'], 'L0_ffn_sh_gate_w': _L0_ffn_in['sh_gate_w'], 'L0_ffn_sh_up_w': _L0_ffn_in['sh_up_w'], 'L0_ffn_sh_down_w': _L0_ffn_in['sh_down_w'], 'L0_c': _L0_c, 'L0_wmod': _L0_wmod}
    _x0 = _d['L0_attn_x']
    _d['L0_attn_x'] = jax.random.normal(jax.random.fold_in(jax.random.key(seed), 1), (1, 2048, 128), dtype=_x0.dtype)
    del _x0
    return _d

def reference(L0_attn_x, L0_attn_in_proj_w, L0_attn_conv_w, L0_attn_conv_b, L0_attn_x_proj_w, L0_attn_dt_proj_w, L0_attn_dt_proj_b, L0_attn_A_log, L0_attn_D, L0_attn_out_proj_w, L0_ffn_router_w, L0_ffn_bias, L0_ffn_gate_w, L0_ffn_up_w, L0_ffn_down_w, L0_ffn_sh_gate_w, L0_ffn_sh_up_w, L0_ffn_sh_down_w, L0_c, L0_wmod):

    def _L0_attn_ref(x, in_proj_w, conv_w, conv_b, x_proj_w, dt_proj_w, dt_proj_b, A_log, D, out_proj_w):
        import jax, jax.numpy as jnp
        import numpy as np
        from jax import lax
        B, L, D_MODEL = (2, 256, 128)
        D_INNER, D_STATE, DT_RANK, D_CONV = (256, 16, 64, 4)

        def _silu(v):
            return v * jax.nn.sigmoid(v)

        def _mamba_forward(x, in_proj_w, conv_w, conv_b, x_proj_w, dt_proj_w, dt_proj_b, A_log, D, out_proj_w):
            b, l, _ = x.shape
            xr = jnp.einsum('bld,ed->ble', x, in_proj_w)
            xs, res = jnp.split(xr, 2, axis=-1)
            xc = jnp.transpose(xs, (0, 2, 1))
            xc = lax.conv_general_dilated(xc, conv_w, window_strides=(1,), padding=[(D_CONV - 1, 0)], feature_group_count=D_INNER, dimension_numbers=('NCH', 'OIH', 'NCH')) + conv_b[None, :, None]
            u = _silu(jnp.transpose(xc, (0, 2, 1)))
            A = -jnp.exp(A_log)
            x_dbl = jnp.einsum('bld,ed->ble', u, x_proj_w)
            dt, Bm, Cm = jnp.split(x_dbl, [DT_RANK, DT_RANK + D_STATE], axis=-1)
            delta = jax.nn.softplus(jnp.einsum('blr,dr->bld', dt, dt_proj_w) + dt_proj_b)
            deltaA = jnp.exp(jnp.einsum('bld,dn->bldn', delta, A))
            deltaBu = jnp.einsum('bld,bln,bld->bldn', delta, Bm, u)

            def step(h, inp):
                dA, dBu, c = inp
                h = dA * h + dBu
                y = jnp.einsum('bdn,bn->bd', h, c)
                return (h, y)
            xs_scan = (jnp.transpose(deltaA, (1, 0, 2, 3)), jnp.transpose(deltaBu, (1, 0, 2, 3)), jnp.transpose(Cm, (1, 0, 2)))
            h0 = jnp.zeros((b, D_INNER, D_STATE), u.dtype)
            _, ys = lax.scan(step, h0, xs_scan)
            y = jnp.transpose(ys, (1, 0, 2)) + u * D
            y = y * _silu(res)
            return jnp.einsum('bld,ed->ble', y, out_proj_w)
        return _mamba_forward(x, in_proj_w, conv_w, conv_b, x_proj_w, dt_proj_w, dt_proj_b, A_log, D, out_proj_w)

    def _L0_ffn_ref(hidden_states, router_w, bias, gate_w, up_w, down_w, sh_gate_w, sh_up_w, sh_down_w):
        import jax, jax.numpy as jnp
        import numpy as np
        B, S, D = (1, 256, 128)
        E, F = (16, 128)
        NG, TKG, K = (4, 2, 4)
        NSH = 2
        SCALE = 2.5
        STD = 0.02
        EPG = E // NG

        def _route(x_flat, router_w, bias):
            logits = x_flat.astype(jnp.float32) @ router_w.T
            scores = jax.nn.sigmoid(logits)
            s = scores + bias[None, :]
            sg = s.reshape(-1, NG, EPG)
            group_score = jax.lax.top_k(sg, 2)[0].sum(-1)
            gidx = jax.lax.top_k(group_score, TKG)[1]
            gmask = jnp.sum(jax.nn.one_hot(gidx, NG, dtype=jnp.float32), axis=1) > 0
            emask = jnp.repeat(gmask, EPG, axis=1)
            masked = jnp.where(emask, s, -1.0)
            topk_idx = jax.lax.top_k(masked, K)[1]
            tw = jnp.take_along_axis(scores, topk_idx, axis=1)
            tw = tw / (tw.sum(-1, keepdims=True) + 1e-20)
            tw = tw * SCALE
            return (topk_idx, tw)
        x = hidden_states.reshape(-1, D)
        topk_idx, tw = _route(x, router_w, bias)
        combine = (jax.nn.one_hot(topk_idx, E, dtype=tw.dtype) * tw[..., None]).sum(1)
        h = jnp.einsum('td,edf->etf', x, gate_w)
        u = jnp.einsum('td,edf->etf', x, up_w)
        y = jnp.einsum('etf,efd->etd', jax.nn.silu(h) * u, down_w)
        routed = jnp.einsum('etd,te->td', y, combine)
        sh = jax.nn.silu(x @ sh_gate_w) * (x @ sh_up_w) @ sh_down_w
        return (routed + sh).reshape(hidden_states.shape)
    x = L0_attn_x
    mod = (_silu(L0_c) @ L0_wmod).reshape(L0_c.shape[0], 6, 1, -1)
    sa, ca, ga, sb, cb, gb = (mod[:, 0], mod[:, 1], mod[:, 2], mod[:, 3], mod[:, 4], mod[:, 5])
    ga = (2 * (ga >= 0) - 1) * jnp.maximum(jnp.abs(ga), 0.25)
    gb = (2 * (gb >= 0) - 1) * jnp.maximum(jnp.abs(gb), 0.25)
    h = _layernorm(x, axis=-1) * (1 + ca) + sa
    x = x + ga * _L0_attn_ref(h, L0_attn_in_proj_w, L0_attn_conv_w, L0_attn_conv_b, L0_attn_x_proj_w, L0_attn_dt_proj_w, L0_attn_dt_proj_b, L0_attn_A_log, L0_attn_D, L0_attn_out_proj_w)
    h = _layernorm(x, axis=-1) * (1 + cb) + sb
    x = x + gb * _L0_ffn_ref(h, L0_ffn_router_w, L0_ffn_bias, L0_ffn_gate_w, L0_ffn_up_w, L0_ffn_down_w, L0_ffn_sh_gate_w, L0_ffn_sh_up_w, L0_ffn_sh_down_w)
    return x

_drawn_inputs = setup_inputs


def setup_inputs(seed=0):
    import zlib

    import numpy as np

    out = dict(_drawn_inputs(seed))
    spreads = {'L0_attn_D': (1.0, 0.6), 'L0_ffn_bias': (0.0, 0.8)}
    factors = {'L0_attn_in_proj_w': 8.0,
     'L0_attn_conv_w': 8.0,
     'L0_attn_conv_b': 8.0,
     'L0_attn_x_proj_w': 8.0,
     'L0_attn_dt_proj_b': 8.0,
     'L0_attn_A_log': 8.0,
     'L0_attn_out_proj_w': 8.0,
     'L0_ffn_router_w': 8.0,
     'L0_ffn_gate_w': 8.0,
     'L0_ffn_up_w': 8.0,
     'L0_ffn_down_w': 8.0,
     'L0_ffn_sh_gate_w': 8.0,
     'L0_ffn_sh_up_w': 8.0,
     'L0_ffn_sh_down_w': 8.0,
     'L0_c': 8.0,
     'L0_wmod': 8.0}
    for name, (base, spread) in spreads.items():
        noise = np.random.default_rng([zlib.crc32(name.encode()), seed]).standard_normal(out[name].shape)
        drawn = base * np.exp(spread * noise) if base else spread * noise
        out[name] = jnp.asarray(drawn.astype(out[name].dtype))
    for name, factor in factors.items():
        out[name] = (out[name] * factor).astype(out[name].dtype)
    return out
```

```python
P = 128
SEQ, DM = 2048, 128
TOK = 512
CHUNKS = SEQ // TOK
DI, NS, RANK, TAPS = 256, 16, 64, 4
TILES = DI // P
CH = P // NS
GROUPS = DI // CH
QUAD = 32
PARTS = 3
ROWS = PARTS * QUAD
NQ = P // QUAD
NJ = QUAD // CH
BLOCK = NQ
BLOCKS = GROUPS // BLOCK
EXPERTS, SHARED, NG, TOPG, TOPK = 16, 2, 4, 2, 4
EPG = EXPERTS // NG
UNITS = EXPERTS + SHARED
SUB = TOK // P
EPS = 1e-5
ROUTE_SCALE = 2.5
A_RING, H_RING, HC_RING = 8, 8, 8

FRONT_PE = ["mean", "var", "in0", "in1", "in2", "in3", "dt", "B", "C", "pre0", "pre1"]
FRONT_ACT = ["sq", "lnv", "rstd", "halo", "xs0", "xs1", "zt0", "zt1", "ut0", "ut1", "dt", "B", "C",
             "abs0", "relu0", "exp0", "one0", "ln0", "abs1", "relu1", "exp1", "one1", "ln1",
             "hi_delta", "mid_delta", "hi_du", "mid_du"]
FRONT_DVE = ["xc", "xn", "h", "conv00", "conv01", "conv02", "conv03", "conv10", "conv11", "conv12", "conv13",
             "z0", "z1", "u0", "u1", "res0", "log0", "delta0", "res1", "log1", "delta1", "du",
             "rem_delta", "lo_delta"]
FRONT_POOL = ["rem_du", "lo_du"]
MID_PE = ["out", "mean", "var", "logits", "combineT"]
MID_ACT = ["sq", "lnv", "rstd", "explog"]
MID_DVE = ["x2", "xc", "xn", "h", "combine", "hi", "rem", "mid", "midrow", "lo"]
ROUTER_STEPS = 44


class Steps:

    def __init__(self, sem, names):
        self.sem, self.names = sem, names

    def done(self, chunk, name):
        return chunk * len(self.names) + (self.names.index(name) + 1)


def wait(engine, sem, value):
    if isinstance(value, int) and value <= 0:
        return
    engine.wait_ge(sem, value)


def build(nc, mybir, ExitStack, t):
    F32, BF16 = mybir.dt.float32, mybir.dt.bfloat16
    ALU, ACT, AX = mybir.AluOpType, mybir.ActivationFunctionType, mybir.AxisListType
    ctx = ExitStack()
    with ctx:
        def sb(name, shape, dt=F32):
            return ctx.enter_context(nc.sbuf_tensor(name, shape, dt))

        def sem(name):
            return ctx.enter_context(nc.semaphore(name))

        x = sb("x", [P, SEQ])
        w_in = sb("w_in", [P, 2 * DI])
        w_dt = sb("w_dt", [P, TILES, P])
        w_B = sb("w_B", [P, TILES, P])
        w_C = sb("w_C", [P, TILES, P])
        w_dtp = sb("w_dtp", [P, DI])
        w_out = sb("w_out", [P, TILES, P])
        small = sb("small", [P, TILES * (TAPS + 3)])
        conv_w = small[:, 0:TILES * TAPS].rearrange("p (m k) -> p m k", k=TAPS)
        conv_b = small[:, TILES * TAPS:TILES * (TAPS + 1)]
        dt_b = small[:, TILES * (TAPS + 1):TILES * (TAPS + 2)]
        skip_D = small[:, TILES * (TAPS + 2):]
        conv_wh = sb("conv_wh", [P, TILES, TAPS])
        conv_bh = sb("conv_bh", [P, TILES])
        A_log = sb("A_log", [P, GROUPS])
        A_neg = sb("A_neg", [P, GROUPS])
        w_router = sb("w_router", [P, EXPERTS])
        r_bias = sb("r_bias", [P, EXPERTS])
        w_gate = sb("w_gate", [P, UNITS, P])
        w_up = sb("w_up", [P, UNITS, P])
        w_down = sb("w_down", [P, UNITS, P])
        ones = sb("ones", [P, P])
        ident = sb("ident", [P, P])
        tri = sb("tri", [P, EXPERTS, EXPERTS])
        tri_g = sb("tri_g", [P, NG, NG])
        pick = sb("pick", [P, NJ, P], BF16)
        gather = sb("gather", [P, NJ, QUAD])
        pick_e = sb("pick_e", [P, EXPERTS, P], BF16)
        eps = sb("eps", [P, 1])
        cvec = sb("cvec", [P, 4])
        mod = sb("mod", [P, 6])
        scale1 = sb("scale1", [P, 8])
        xc1 = sb("xc1", [P, TOK])
        sq1 = sb("sq1", [P, TOK])
        h1 = sb("h1", [P, TOK])
        xs = sb("xs", [P, TILES, TOK + TAPS - 1])
        u = sb("u", [P, TILES, TOK])
        z = sb("z", [P, TILES, TOK])
        dt = sb("dt", [P, TOK])
        B_bc = sb("B_bc", [P, TOK])
        C_bc = sb("C_bc", [P, TOK])
        delta = sb("delta", [P, TILES, TOK])
        du = sb("du", [P, TILES, TOK])
        parts = sb("parts", [P, 2, PARTS, TILES, TOK], BF16)
        stack = sb("stack", [P, 2, NQ, TILES, TOK], BF16)
        a = sb("a", [P, A_RING, TOK])
        dbu = sb("dbu", [P, 2, TOK])
        h = sb("h", [P, H_RING, TOK])
        hc = sb("hc", [P, HC_RING, TOK])
        state = sb("state", [P, GROUPS])
        yg = sb("yg", [P, TILES, TOK])
        sp = hc[:, :, :].rearrange("p (m k) t -> p m k t", k=4)
        rem = h[:, 0:4, :].rearrange("p (k m) t -> p k m t", k=2)
        cv = dbu
        w_mod = hc[:, 0:2, 0:3 * P]
        x2 = sb("x2", [P, TOK])
        xc2 = sb("xc2", [P, TOK])
        sq2 = sb("sq2", [P, TOK])
        h2 = sb("h2", [P, TOK])
        score = sb("score", [P, SUB, EXPERTS])
        sel = sb("sel", [P, SUB, EXPERTS])
        comb = sb("comb", [P, SUB, EXPERTS])
        rt = sb("rt", [P, 8, SUB * EXPERTS])
        gpair = sb("gpair", [P, 2, SUB * NG * NG])
        pair = sb("pair", [P, 2, EXPERTS, EXPERTS])
        cstack = sb("cstack", [P, TOK], BF16)
        crem = sb("crem", [NS, TOK])
        cmid = sb("cmid", [NS, TOK], BF16)
        th = sb("th", [P, 2, TOK])
        sg = sb("sg", [P, 2, TOK])
        cb = sb("cb", [P, 2, TOK])
        sc = sb("sc", [P, 2, TOK])
        act_o = sb("act_o", [P, 2, TOK])

        bank = [ctx.enter_context(nc.psum_tensor(f"bank{i}", [P, TOK], F32)) for i in range(8)]
        ps_delta, ps_du, ps_y, ps_acc, ps_g, ps_u, ps_cb = bank[0:2], bank[2], bank[3], bank[4], bank[5], bank[6], bank[7]

        front_pe = Steps(sem("front_pe"), FRONT_PE)
        front_act = Steps(sem("front_act"), FRONT_ACT)
        front_dve = Steps(sem("front_dve"), FRONT_DVE)
        front_pool = Steps(sem("front_pool"), FRONT_POOL)
        mid_pe = Steps(sem("mid_pe"), MID_PE)
        mid_act = Steps(sem("mid_act"), MID_ACT)
        mid_dve = Steps(sem("mid_dve"), MID_DVE)
        router = sem("router")
        x_in, w_a, w_b, w_c = sem("x_in"), sem("w_a"), sem("w_b"), sem("w_c")
        setup_dve, setup_act, setup_pe = sem("setup_dve"), sem("setup_act"), sem("setup_pe")
        delta_in, du_in = sem("delta_in"), sem("du_in")
        delta_bc, du_bc, a_ready, dbu_ready = sem("delta_bc"), sem("du_bc"), sem("a_ready"), sem("dbu_ready")
        h_ready, state_saved, hc_ready, y_added = sem("h_ready"), sem("state_saved"), sem("hc_ready"), sem("y_added")
        y_read, yg_ready = sem("y_read"), sem("yg_ready")
        cb_ps, g_ps, u_ps, down = sem("cb_ps"), sem("g_ps"), sem("u_ps"), sem("down")
        cb_ready, th_ready, sg_ready, sc_ready, act_ready = sem("cb_ready"), sem("th_ready"), sem("sg_ready"), sem("sc_ready"), sem("act_ready")
        out_ready, out_done = sem("out_ready"), sem("out_done")
        SETUP_DVE = 16

        def cols(c):
            return slice(c * TOK, (c + 1) * TOK)

        def xcols(c):
            return x[:, bass_ds(c * TOK, TOK)]

        bass_ds = t["ds"]
        BIG_LOADS = [(w_gate, "w_gate"), (w_up, "w_up"), (w_down, "w_down")]
        FRONT_LOADS = [(w_in, "w_in"), (w_dt, "w_dt"), (w_B, "w_B"), (w_C, "w_C"), (w_dtp, "w_dtp"), (ones, "ones"),
                       (small, "small"), (A_log, "A_log"), (pick, "pick"), (gather, "gather"), (w_mod, "w_mod"),
                       (cvec[:, 0:1], "cvec")]
        MID_LOADS = [(w_out, "w_out"), (w_router, "w_router"), (r_bias, "r_bias"), (ident, "ident"), (tri, "tri"),
                     (tri_g, "tri_g"), (pick_e, "pick_e")]

        with nc.Block() as block:

            @block.sync
            def _(sp_eng):
                sp_eng.dma_start(x[:, 0:TOK], t["x"][:, 0:TOK]).then_inc(x_in, 16)
                for dst, name in FRONT_LOADS:
                    sp_eng.dma_start(dst[:], t[name]).then_inc(w_a, 16)
                sp_eng.wait_ge(x_in, 16)
                sp_eng.dma_start(x[:, TOK:], t["x"][:, TOK:]).then_inc(x_in, 16)
                for dst, name in MID_LOADS:
                    sp_eng.dma_start(dst[:], t[name]).then_inc(w_b, 16)
                for dst, name in BIG_LOADS:
                    sp_eng.dma_start(dst[:], t[name]).then_inc(w_c, 16)

                def restack(c):
                    ready = [[(front_act, "hi_delta"), (front_act, "mid_delta"), (front_dve, "lo_delta")],
                             [(front_act, "hi_du"), (front_act, "mid_du"), (front_pool, "lo_du")]]
                    wait(sp_eng, du_bc, c * GROUPS)
                    for kind, arrived in enumerate([delta_in, du_in]):
                        for part in range(PARTS):
                            stage, step = ready[kind][part]
                            sp_eng.wait_ge(stage.sem, stage.done(c, step))
                            for q in range(NQ):
                                sp_eng.dma_start(stack[QUAD * part:QUAD * (part + 1), kind, q],
                                                 parts[QUAD * q:QUAD * (q + 1), kind, part]).then_inc(arrived, 16)

                def store(f):
                    sp_eng.wait_ge(out_ready, f + 2)
                    sp_eng.dma_start(t["out"][:, bass_ds(f * TOK, TOK)], x2[:]).then_inc(out_done, 16)

                restack(0)
                with sp_eng.Fori(1, CHUNKS) as c:
                    restack(c)
                    store(c - 1)
                store(CHUNKS - 1)
                sp_eng.wait_ge(out_done, 16 + 16 * CHUNKS)

            @block.tensor
            def _(pe):
                def mm(out, lhsT, rhs, start=True, stop=True):
                    return nc.tensor.matmul(out, lhsT, rhs, start=start, stop=stop)

                def front_a(c):
                    pe.wait_ge(x_in, 16 if isinstance(c, int) else 32)
                    mm(ps_g[:], ones[:], xcols(c)).then_inc(front_pe.sem, 1)

                def front_b(c):
                    pe.wait_ge(front_act.sem, front_act.done(c, "sq"))
                    mm(ps_u[:], ones[:], sq1[:]).then_inc(front_pe.sem, 1)

                def front_c(c):
                    pe.wait_ge(front_dve.sem, front_dve.done(c, "h"))
                    for m, dst in enumerate([ps_g, ps_u, ps_cb, ps_g]):
                        if m == 1:
                            pe.wait_ge(front_act.sem, front_act.done(c, "lnv"))
                        if m == 3:
                            pe.wait_ge(front_act.sem, front_act.done(c, "xs0"))
                        mm(dst[:], w_in[:, m * P:(m + 1) * P], h1[:]).then_inc(front_pe.sem, 1)

                def front_d(c):
                    pe.wait_ge(front_dve.sem, front_dve.done(c, "u1"))
                    for w, dst in ((w_dt, ps_u), (w_B, ps_cb), (w_C, ps_g)):
                        for m in range(TILES):
                            last = mm(dst[:], w[:, m], u[:, m], start=m == 0, stop=m == TILES - 1)
                        last.then_inc(front_pe.sem, 1)
                    for m, (dst, step) in enumerate(((ps_u, "dt"), (ps_cb, "B"))):
                        pe.wait_ge(front_act.sem, front_act.done(c, step))
                        mm(dst[:], w_dtp[:, m * P:(m + 1) * P], dt[:]).then_inc(front_pe.sem, 1)

                def mid_a(f):
                    pe.wait_ge(yg_ready, TILES * f + TILES)
                    pe.wait_ge(out_ready, f + 1)
                    for m in range(TILES):
                        last = mm(ps_acc[:], w_out[:, m], yg[:, m], start=m == 0, stop=m == TILES - 1)
                    last.then_inc(mid_pe.sem, 1)

                def mid_b(f):
                    pe.wait_ge(mid_dve.sem, mid_dve.done(f, "x2"))
                    mm(ps_acc[:], ones[:], x2[:]).then_inc(mid_pe.sem, 1)

                def mid_c(f):
                    pe.wait_ge(mid_act.sem, mid_act.done(f, "sq"))
                    mm(ps_acc[:], ones[:], sq2[:]).then_inc(mid_pe.sem, 1)

                def mid_d(f):
                    pe.wait_ge(mid_dve.sem, mid_dve.done(f, "h"))
                    for s in range(SUB):
                        last = mm(ps_acc[:, s * EXPERTS:(s + 1) * EXPERTS], h2[:, s * P:(s + 1) * P], w_router[:])
                    last.then_inc(mid_pe.sem, 1)

                def mid_e(f):
                    pe.wait_ge(mid_dve.sem, mid_dve.done(f, "combine"))
                    for s in range(SUB):
                        last = nc.tensor.transpose(ps_acc[0:EXPERTS, s * P:(s + 1) * P], comb[:, s], ident[:])
                    last.then_inc(mid_pe.sem, 1)

                def broadcast(c, g):
                    tile, q, j = g // (GROUPS // TILES), g % NQ, g // NQ % NJ
                    wait(pe, a_ready, c * GROUPS + g - 1)
                    mm(ps_delta[g % 2][:], pick[0:ROWS, j], stack[0:ROWS, 0, q, tile]).then_inc(delta_bc, 1)
                    wait(pe, dbu_ready, c * GROUPS + g)
                    mm(ps_du[:], pick[0:ROWS, j], stack[0:ROWS, 1, q, tile]).then_inc(du_bc, 1)

                def add_states(c, b):
                    j = b % NJ
                    pe.wait_ge(hc_ready, c * GROUPS + BLOCK * (b + 1))
                    if j == 0:
                        wait(pe, y_read, c * TILES + b // NJ)
                    for q in range(NQ):
                        last = mm(ps_y[QUAD * q:QUAD * (q + 1), :], gather[:, j], hc[:, (BLOCK * b + q) % HC_RING],
                                  start=j == 0, stop=j == NJ - 1)
                    last.then_inc(y_added, 1)

                def unit(f, e, front_there):
                    if e < EXPERTS:
                        if e == 0:
                            pe.wait_ge(mid_dve.sem, mid_dve.done(f, "lo"))
                            if front_there:
                                pe.wait_ge(front_act.sem, front_act.done(f + 1, "relu1"))
                        else:
                            pe.wait_ge(cb_ready, f * EXPERTS + e)
                        mm(ps_cb[:], pick_e[:, e], cstack[:]).then_inc(cb_ps, 1)
                    if e:
                        pe.wait_ge(sg_ready, f * UNITS + e)
                    mm(ps_g[:], w_gate[:, e], h2[:]).then_inc(g_ps, 1)
                    if e:
                        pe.wait_ge(act_ready, f * UNITS + e)
                    mm(ps_u[:], w_up[:, e], h2[:]).then_inc(u_ps, 1)
                    if e:
                        mm(ps_acc[:], w_down[:, e - 1], act_o[:, (e - 1) % 2], start=e == 1, stop=False).then_inc(down, 1)

                def last_down(f):
                    pe.wait_ge(act_ready, (f + 1) * UNITS)
                    mm(ps_acc[:], w_down[:, UNITS - 1], act_o[:, (UNITS - 1) % 2], start=False).then_inc(down, 1)

                def iteration(c, scan=True, ffn=True):
                    f = c - 1
                    if scan:
                        front_a(c)
                    if ffn:
                        mid_a(f)
                    if scan:
                        front_b(c)
                    if ffn:
                        mid_b(f)
                        mid_c(f)
                    if scan:
                        front_c(c)
                        front_d(c)
                    if ffn:
                        mid_d(f)
                        mid_e(f)
                    if scan:
                        pe.wait_ge(delta_in, 16 * PARTS * NQ * c + 16 * PARTS * NQ)
                        pe.wait_ge(du_in, 16 * PARTS * NQ * c + 16 * PARTS * NQ)
                        for g in range(GROUPS):
                            broadcast(c, g)
                            if ffn and unit_at(g) is not None:
                                unit(f, unit_at(g), True)
                            if g % BLOCK == BLOCK - 1 and g >= 2 * BLOCK - 1:
                                add_states(c, g // BLOCK - 1)
                        add_states(c, BLOCKS - 1)
                    elif ffn:
                        for e in range(UNITS):
                            unit(f, e, False)
                    if ffn:
                        last_down(f)

                pe.wait_ge(w_a, 16 * len(FRONT_LOADS))
                pe.wait_ge(setup_dve, 3)
                for k in range(6):
                    last = mm(ps_acc[:, k:k + 1], w_mod[:, k // 3, (k % 3) * P:(k % 3 + 1) * P], cvec[:, 3:4])
                last.then_inc(setup_pe, 1)
                iteration(0, ffn=False)
                pe.wait_ge(w_b, 16 * len(MID_LOADS))
                pe.wait_ge(w_c, 16 * len(BIG_LOADS))
                with pe.Fori(1, CHUNKS) as c:
                    iteration(c)
                iteration(CHUNKS, scan=False)

            @block.scalar
            def _(act):
                def ln_exp_set():
                    nc.scalar.preload_act_table_set("natural_log_exp_and_others")

                def exp_tanh_set():
                    nc.scalar.preload_act_table_set("exp_and_others")

                def front_a(c):
                    act.wait_ge(front_dve.sem, front_dve.done(c, "xc"))
                    wait(act, front_pe.sem, front_pe.done(c - 1, "var"))
                    nc.scalar.activation(sq1[:], xc1[:], ACT.Square).then_inc(front_act.sem, 1)
                    act.wait_ge(front_pe.sem, front_pe.done(c, "var"))
                    nc.scalar.activation(sq1[:], ps_u[:], ACT.Ln, bias=eps[:]).then_inc(front_act.sem, 1)
                    act.wait_ge(front_act.sem, front_act.done(c, "lnv"))
                    nc.scalar.activation(sq1[:], sq1[:], ACT.Exp, scale=-0.5).then_inc(front_act.sem, 1)

                def front_b(c):
                    wait(act, front_dve.sem, front_dve.done(c - 1, "conv13"))
                    wait(act, front_act.sem, front_act.done(c - 1, "xs1"))
                    nc.scalar.copy(xs[:, :, 0:TAPS - 1], xs[:, :, TOK:]).then_inc(front_act.sem, 1)
                    act.wait_ge(front_act.sem, front_act.done(c, "halo"))
                    for m, src in enumerate((ps_g, ps_u)):
                        act.wait_ge(front_pe.sem, front_pe.done(c, f"in{m}"))
                        nc.scalar.copy(xs[:, m, TAPS - 1:], src[:]).then_inc(front_act.sem, 1)
                    wait(act, yg_ready, TILES * c)
                    for m, src in enumerate((ps_cb, ps_g)):
                        act.wait_ge(front_pe.sem, front_pe.done(c, f"in{m + 2}"))
                        nc.scalar.activation(z[:, m], src[:], ACT.Tanh, scale=0.5).then_inc(front_act.sem, 1)
                    for m in range(TILES):
                        act.wait_ge(front_dve.sem, front_dve.done(c, f"conv{m}3"))
                        nc.scalar.activation(u[:, m], cv[:, m], ACT.Tanh).then_inc(front_act.sem, 1)

                def front_c(c):
                    act.wait_ge(front_pe.sem, front_pe.done(c, "dt"))
                    nc.scalar.copy(dt[:], ps_u[:]).then_inc(front_act.sem, 1)
                    wait(act, dbu_ready, GROUPS * c)
                    act.wait_ge(front_pe.sem, front_pe.done(c, "B"))
                    nc.scalar.copy(B_bc[:], ps_cb[:]).then_inc(front_act.sem, 1)
                    wait(act, hc_ready, GROUPS * c)
                    act.wait_ge(front_pe.sem, front_pe.done(c, "C"))
                    nc.scalar.copy(C_bc[:], ps_g[:]).then_inc(front_act.sem, 1)

                def front_d(c):
                    wait(act, y_added, BLOCKS * c)
                    for m, src in enumerate((ps_u, ps_cb)):
                        v_exp, v_one, v_ln, v_relu = (sp[:, m, k] for k in range(4))
                        act.wait_ge(front_pe.sem, front_pe.done(c, f"pre{m}"))
                        nc.scalar.activation(v_exp, src[:], ACT.Abs, bias=dt_b[:, m:m + 1]).then_inc(front_act.sem, 1)
                        nc.scalar.activation(v_relu, src[:], ACT.Relu, bias=dt_b[:, m:m + 1]).then_inc(front_act.sem, 1)
                        act.wait_ge(front_act.sem, front_act.done(c, f"abs{m}"))
                        nc.scalar.activation(v_exp, v_exp, ACT.Exp, scale=-1.0).then_inc(front_act.sem, 1)
                        act.wait_ge(front_act.sem, front_act.done(c, f"exp{m}"))
                        nc.scalar.activation(v_one, v_exp, ACT.Identity, bias=1.0).then_inc(front_act.sem, 1)
                        nc.scalar.activation(v_ln, v_exp, ACT.Ln, bias=1.0).then_inc(front_act.sem, 1)
                    wait(act, delta_in, 16 * PARTS * NQ * c)
                    act.wait_ge(front_dve.sem, front_dve.done(c, "delta1"))
                    nc.scalar.copy(parts[:, 0, 0], delta[:]).then_inc(front_act.sem, 1)
                    act.wait_ge(front_dve.sem, front_dve.done(c, "rem_delta"))
                    nc.scalar.copy(parts[:, 0, 1], rem[:, 0]).then_inc(front_act.sem, 1)
                    wait(act, du_in, 16 * PARTS * NQ * c)
                    act.wait_ge(front_dve.sem, front_dve.done(c, "du"))
                    nc.scalar.copy(parts[:, 1, 0], du[:]).then_inc(front_act.sem, 1)
                    act.wait_ge(front_pool.sem, front_pool.done(c, "rem_du"))
                    nc.scalar.copy(parts[:, 1, 1], rem[:, 1]).then_inc(front_act.sem, 1)

                def mid_a(f):
                    act.wait_ge(mid_dve.sem, mid_dve.done(f, "xc"))
                    nc.scalar.activation(sq2[:], xc2[:], ACT.Square).then_inc(mid_act.sem, 1)

                def mid_b(f):
                    act.wait_ge(mid_pe.sem, mid_pe.done(f, "var"))
                    nc.scalar.activation(sq2[:], ps_acc[:], ACT.Ln, bias=eps[:]).then_inc(mid_act.sem, 1)
                    act.wait_ge(mid_act.sem, mid_act.done(f, "lnv"))
                    nc.scalar.activation(sq2[:], sq2[:], ACT.Exp, scale=-0.5).then_inc(mid_act.sem, 1)

                def mid_c(f):
                    act.wait_ge(mid_pe.sem, mid_pe.done(f, "logits"))
                    nc.scalar.activation(rt[:, 0], ps_acc[:, 0:SUB * EXPERTS], ACT.Exp, scale=-1.0).then_inc(mid_act.sem, 1)

                def decay(c, g):
                    act.wait_ge(delta_bc, c * GROUPS + g + 1)
                    wait(act, h_ready, c * GROUPS + g + 1 - A_RING)
                    nc.scalar.activation(a[:, g % A_RING], ps_delta[g % 2][:], ACT.Exp,
                                         scale=A_neg[:, g:g + 1]).then_inc(a_ready, 1)

                def unit(f, e):
                    if e < EXPERTS:
                        act.wait_ge(cb_ps, f * EXPERTS + e + 1)
                        if e >= 2:
                            act.wait_ge(sc_ready, f * EXPERTS + e - 1)
                        nc.scalar.copy(cb[:, e % 2], ps_cb[:]).then_inc(cb_ready, 1)
                    act.wait_ge(g_ps, f * UNITS + e + 1)
                    if e >= 2:
                        act.wait_ge(sg_ready, f * UNITS + e - 1)
                    nc.scalar.activation(th[:, e % 2], ps_g[:], ACT.Tanh, scale=0.5).then_inc(th_ready, 1)

                def iteration(c, scan=True, ffn=True):
                    f = c - 1
                    ln_exp_set()
                    if scan:
                        front_a(c)
                    if ffn:
                        mid_a(f)
                        mid_b(f)
                    exp_tanh_set()
                    if scan:
                        front_b(c)
                        front_c(c)
                    if ffn:
                        mid_c(f)
                    if scan:
                        ln_exp_set()
                        front_d(c)
                        exp_tanh_set()
                        for g in range(GROUPS):
                            decay(c, g)
                            if ffn and unit_at(g) is not None:
                                unit(f, unit_at(g))
                    elif ffn:
                        for e in range(UNITS):
                            unit(f, e)

                exp_tanh_set()
                act.wait_ge(w_a, 16 * len(FRONT_LOADS))
                nc.scalar.activation(cvec[:, 1:2], cvec[:, 0:1], ACT.Exp, scale=-1.0).then_inc(setup_act, 1)
                nc.scalar.activation(A_neg[:], A_log[:], ACT.Exp).then_inc(setup_act, 1)
                act.wait_ge(setup_act, 2)
                nc.scalar.mul(A_neg[:], A_neg[:], -1.0).then_inc(setup_act, 1)
                act.wait_ge(setup_pe, 1)
                nc.scalar.copy(mod[:], ps_acc[:, 0:6]).then_inc(setup_act, 1)
                act.wait_ge(setup_act, 4)
                act.wait_ge(setup_dve, SETUP_DVE)
                iteration(0, ffn=False)
                with act.Fori(1, CHUNKS) as c:
                    iteration(c)
                iteration(CHUNKS, scan=False)

            @block.gpsimd
            def _(pool):
                def front(c):
                    pool.wait_ge(front_act.sem, front_act.done(c, "hi_du"))
                    wait(pool, hc_ready, GROUPS * c)
                    wait(pool, state_saved, BLOCKS * c)
                    nc.gpsimd.tensor_sub(rem[:, 1], du[:], parts[:, 1, 0]).then_inc(front_pool.sem, 1)
                    pool.wait_ge(front_act.sem, front_act.done(c, "mid_du"))
                    nc.gpsimd.tensor_sub(parts[:, 1, 2], rem[:, 1], parts[:, 1, 1]).then_inc(front_pool.sem, 1)

                def times_C(c, g):
                    pool.wait_ge(h_ready, c * GROUPS + g + 1)
                    wait(pool, y_added, c * BLOCKS + g // BLOCK - 1)
                    nc.gpsimd.tensor_mul(hc[:, g % HC_RING], h[:, g % H_RING], C_bc[:]).then_inc(hc_ready, 1)

                def unit(f, e):
                    pool.wait_ge(sg_ready, f * UNITS + e + 1)
                    pool.wait_ge(cb_ready, f * EXPERTS + e + 1)
                    if e >= 2:
                        pool.wait_ge(act_ready, f * UNITS + e - 1)
                    nc.gpsimd.tensor_mul(sc[:, e % 2], sg[:, e % 2], cb[:, e % 2]).then_inc(sc_ready, 1)

                def iteration(c, scan=True, ffn=True):
                    f = c - 1
                    if scan:
                        front(c)
                        pool.wait_ge(front_act.sem, front_act.done(c, "C"))
                        for g in range(GROUPS):
                            times_C(c, g)
                            e = unit_at(g)
                            if ffn and e is not None and e < EXPERTS:
                                unit(f, e)
                    elif ffn:
                        for e in range(EXPERTS):
                            unit(f, e)

                iteration(0, ffn=False)
                with pool.Fori(1, CHUNKS) as c:
                    iteration(c)
                iteration(CHUNKS, scan=False)

            @block.vector
            def _(dve):
                V = nc.vector
                one_ca, one_cb, ga_half, gb = (scale1[:, k:k + 1] for k in range(4))
                sa, sb_ = mod[:, 0:1], mod[:, 3:4]

                def setup():
                    n = [0]

                    def link(ins):
                        n[0] += 1
                        ins.then_inc(setup_dve, 1)
                        dve.wait_ge(setup_dve, n[0])

                    dve.wait_ge(setup_act, 1)
                    link(V.tensor_scalar(cvec[:, 2:3], cvec[:, 1:2], 1.0, None, ALU.add))
                    link(V.reciprocal(cvec[:, 1:2], cvec[:, 2:3]))
                    link(V.tensor_mul(cvec[:, 3:4], cvec[:, 0:1], cvec[:, 1:2]))
                    V.memset(eps[:], EPS)
                    V.memset(xs[:], 0.0)
                    V.memset(cstack[:], 0.0)
                    link(V.memset(state[:], 0.0))
                    link(V.tensor_scalar(conv_wh[:], conv_w, 0.5, None, ALU.mult))
                    link(V.tensor_scalar(conv_bh[:], conv_b, 0.5, None, ALU.mult))
                    dve.wait_ge(setup_act, 4)
                    link(V.tensor_scalar(one_ca, mod[:, 1:2], 1.0, None, ALU.add))
                    link(V.tensor_scalar(one_cb, mod[:, 4:5], 1.0, None, ALU.add))
                    for dst, k, sign in ((ga_half, 2, 1.0), (gb, 5, 2.0)):
                        link(V.tensor_scalar(scale1[:, 4:5], mod[:, k:k + 1], 0.0, sign, ALU.is_ge, ALU.mult))
                        link(V.scalar_tensor_tensor(scale1[:, 7:8], mod[:, k:k + 1], -1.0, mod[:, k:k + 1], ALU.mult, ALU.max))
                        V.tensor_scalar(scale1[:, 5:6], scale1[:, 7:8], 0.25, None, ALU.max)
                        link(V.tensor_scalar(scale1[:, 6:7], scale1[:, 4:5], sign / 2, None, ALU.subtract))
                        if k == 2:
                            link(V.tensor_mul(dst, scale1[:, 6:7], scale1[:, 5:6]))
                        else:
                            V.tensor_mul(dst, scale1[:, 6:7], scale1[:, 5:6]).then_inc(setup_dve, 1)
                    assert n[0] == SETUP_DVE - 1, n
                    dve.wait_ge(setup_dve, SETUP_DVE)
                    dve.sem_inc(out_ready, 1)
                    dve.sem_inc(out_done, 16)

                def f_wait(c, step):
                    dve.wait_ge(front_dve.sem, front_dve.done(c, step))

                def front_a(c):
                    dve.wait_ge(front_pe.sem, front_pe.done(c, "mean"))
                    V.tensor_sub(xc1[:], xcols(c), ps_g[:]).then_inc(front_dve.sem, 1)

                def front_b(c):
                    dve.wait_ge(front_act.sem, front_act.done(c, "rstd"))
                    V.tensor_mul(xc1[:], xc1[:], sq1[:]).then_inc(front_dve.sem, 1)
                    f_wait(c, "xn")
                    V.tensor_scalar(h1[:], xc1[:], one_ca, sa, ALU.mult, ALU.add).then_inc(front_dve.sem, 1)

                def front_c(c):
                    for m in range(TILES):
                        dve.wait_ge(front_act.sem, front_act.done(c, f"xs{m}"))
                        V.tensor_scalar(cv[:, m], xs[:, m, 0:TOK], conv_wh[:, m, 0:1], conv_bh[:, m:m + 1],
                                        ALU.mult, ALU.add).then_inc(front_dve.sem, 1)
                        for k in range(1, TAPS):
                            f_wait(c, f"conv{m}{k - 1}")
                            V.scalar_tensor_tensor(cv[:, m], xs[:, m, k:k + TOK], conv_wh[:, m, k:k + 1], cv[:, m],
                                                   ALU.mult, ALU.add).then_inc(front_dve.sem, 1)
                    for m, src in enumerate((ps_cb, ps_g)):
                        dve.wait_ge(front_act.sem, front_act.done(c, f"zt{m}"))
                        V.scalar_tensor_tensor(z[:, m], z[:, m], 1.0, src[:], ALU.add, ALU.mult).then_inc(front_dve.sem, 1)
                    for m in range(TILES):
                        dve.wait_ge(front_act.sem, front_act.done(c, f"ut{m}"))
                        V.scalar_tensor_tensor(u[:, m], u[:, m], 1.0, cv[:, m], ALU.add, ALU.mult).then_inc(front_dve.sem, 1)

                def front_d(c):
                    for m in range(TILES):
                        v_exp, v_one, v_ln, v_relu = (sp[:, m, k] for k in range(4))
                        dve.wait_ge(front_act.sem, front_act.done(c, f"ln{m}"))
                        V.scalar_tensor_tensor(v_one, v_one, 1.0, v_exp, ALU.subtract, ALU.subtract).then_inc(front_dve.sem, 1)
                        f_wait(c, f"res{m}")
                        V.tensor_sub(v_ln, v_ln, v_one).then_inc(front_dve.sem, 1)
                        f_wait(c, f"log{m}")
                        V.tensor_add(delta[:, m], v_ln, v_relu).then_inc(front_dve.sem, 1)
                    f_wait(c, "delta1")
                    wait(dve, front_pool.sem, front_pool.done(c - 1, "rem_du"))
                    V.tensor_mul(du[:], delta[:], u[:]).then_inc(front_dve.sem, 1)
                    dve.wait_ge(front_act.sem, front_act.done(c, "hi_delta"))
                    wait(dve, hc_ready, GROUPS * c)
                    wait(dve, state_saved, BLOCKS * c)
                    V.tensor_sub(rem[:, 0], delta[:], parts[:, 0, 0]).then_inc(front_dve.sem, 1)
                    dve.wait_ge(front_act.sem, front_act.done(c, "mid_delta"))
                    f_wait(c, "rem_delta")
                    V.tensor_sub(parts[:, 0, 2], rem[:, 0], parts[:, 0, 1]).then_inc(front_dve.sem, 1)

                def m_wait(f, step):
                    dve.wait_ge(mid_dve.sem, mid_dve.done(f, step))

                def mid_a(f):
                    dve.wait_ge(mid_pe.sem, mid_pe.done(f, "out"))
                    dve.wait_ge(out_done, 16 * f + 16)
                    V.scalar_tensor_tensor(x2[:], ps_acc[:], ga_half, xcols(f), ALU.mult, ALU.add).then_inc(mid_dve.sem, 1)

                def mid_b(f):
                    dve.wait_ge(mid_pe.sem, mid_pe.done(f, "mean"))
                    m_wait(f, "x2")
                    V.tensor_sub(xc2[:], x2[:], ps_acc[:]).then_inc(mid_dve.sem, 1)

                def mid_c(f):
                    dve.wait_ge(mid_act.sem, mid_act.done(f, "rstd"))
                    V.tensor_mul(xc2[:], xc2[:], sq2[:]).then_inc(mid_dve.sem, 1)
                    m_wait(f, "xn")
                    V.tensor_scalar(h2[:], xc2[:], one_cb, sb_, ALU.mult, ALU.add).then_inc(mid_dve.sem, 1)

                def mid_d(f):
                    n = [0]

                    def link(ins):
                        n[0] += 1
                        ins.then_inc(router, 1)
                        dve.wait_ge(router, f * ROUTER_STEPS + n[0])

                    def bias_like(k):
                        return rt[:, k].rearrange("p (s e) -> p s e", e=EXPERTS)

                    SG = SUB * NG
                    den, biased, masked, best, rank = (bias_like(k) for k in range(5))
                    dve.wait_ge(mid_act.sem, mid_act.done(f, "explog"))
                    link(V.tensor_scalar(den, den, 1.0, None, ALU.add))
                    link(V.reciprocal(score[:], den))
                    link(V.tensor_tensor(biased, score[:], r_bias[:, :].unsqueeze(1).broadcast_to([P, SUB, EXPERTS]), ALU.add))
                    four = rt[:, 1].rearrange("p (g b a) -> p g b a", a=2, b=2)
                    hi2 = rt[:, 5, 0:2 * SG].rearrange("p (g b) -> p g b", b=2)
                    lo2 = rt[:, 6, 0:2 * SG].rearrange("p (g b) -> p g b", b=2)
                    link(V.tensor_tensor(hi2, four[:, :, :, 0], four[:, :, :, 1], ALU.max))
                    link(V.tensor_tensor(lo2, four[:, :, :, 0], four[:, :, :, 1], ALU.min))
                    top1, mid1, low1, gs = (rt[:, 7, k * SG:(k + 1) * SG] for k in range(4))
                    link(V.tensor_tensor(top1, hi2[:, :, 0], hi2[:, :, 1], ALU.max))
                    link(V.tensor_tensor(mid1, hi2[:, :, 0], hi2[:, :, 1], ALU.min))
                    link(V.tensor_tensor(low1, lo2[:, :, 0], lo2[:, :, 1], ALU.max))
                    link(V.tensor_tensor(mid1, mid1, low1, ALU.max))
                    link(V.tensor_tensor(gs, top1, mid1, ALU.add))
                    gs3 = gs.rearrange("p (s g) -> p s g", g=NG)
                    gj = gs3.unsqueeze(2).broadcast_to([P, SUB, NG, NG])
                    gi = gs3.unsqueeze(3).broadcast_to([P, SUB, NG, NG])
                    gt4 = gpair[:, 0].rearrange("p (s i j) -> p s i j", i=NG, j=NG)
                    eq4 = gpair[:, 1].rearrange("p (s i j) -> p s i j", i=NG, j=NG)
                    link(V.tensor_tensor(gt4, gj, gi, ALU.is_gt))
                    link(V.tensor_tensor(eq4, gj, gi, ALU.is_equal))
                    link(V.tensor_tensor(eq4, eq4, tri_g[:, :, :].unsqueeze(1).broadcast_to([P, SUB, NG, NG]), ALU.mult))
                    link(V.tensor_tensor(gt4, gt4, eq4, ALU.add))
                    grank = rt[:, 5, 0:SG]
                    link(V.tensor_reduce(grank, gpair[:, 0].rearrange("p (q j) -> p q j", j=NG), AX.X, ALU.add))
                    link(V.tensor_scalar(grank, grank, float(TOPG), None, ALU.is_lt))
                    gm = grank.unsqueeze(2).broadcast_to([P, SG, EPG])
                    s4 = rt[:, 1].rearrange("p (q e) -> p q e", e=EPG)
                    m4 = rt[:, 2].rearrange("p (q e) -> p q e", e=EPG)
                    link(V.tensor_tensor(m4, s4, gm, ALU.mult))
                    gm1 = rt[:, 6, 0:SG]
                    link(V.tensor_scalar(gm1, grank, 1.0, None, ALU.subtract))
                    link(V.tensor_tensor(m4, m4, gm1.unsqueeze(2).broadcast_to([P, SG, EPG]), ALU.add))
                    for s in range(SUB):
                        ej = masked[:, s].unsqueeze(1).broadcast_to([P, EXPERTS, EXPERTS])
                        ei = masked[:, s].unsqueeze(2).broadcast_to([P, EXPERTS, EXPERTS])
                        V.tensor_tensor(pair[:, 0], ej, ei, ALU.is_gt).then_inc(router, 1)
                        link(V.tensor_tensor(pair[:, 1], ej, ei, ALU.is_equal))
                        n[0] += 1
                        dve.wait_ge(router, f * ROUTER_STEPS + n[0])
                        link(V.tensor_tensor(pair[:, 1], pair[:, 1], tri[:], ALU.mult))
                        link(V.tensor_tensor(pair[:, 0], pair[:, 0], pair[:, 1], ALU.add))
                        link(V.tensor_reduce(rank[:, s], pair[:, 0], AX.X, ALU.add))
                    link(V.tensor_scalar(sel[:], rank, float(TOPK), None, ALU.is_lt))
                    link(V.tensor_tensor(sel[:], sel[:], score[:], ALU.mult))
                    tot = rt[:, 6, 0:SUB]
                    link(V.tensor_reduce(tot, sel[:], AX.X, ALU.add))
                    link(V.tensor_scalar(tot, tot, 1e-20, None, ALU.add))
                    link(V.reciprocal(rt[:, 5, 0:SUB], tot))
                    V.scalar_tensor_tensor(comb[:], sel[:], ROUTE_SCALE / 2,
                                           rt[:, 5, 0:SUB].unsqueeze(2).broadcast_to([P, SUB, EXPERTS]),
                                           ALU.mult, ALU.mult).then_inc(mid_dve.sem, 1)
                    assert n[0] == ROUTER_STEPS, n

                def mid_e(f):
                    dve.wait_ge(mid_pe.sem, mid_pe.done(f, "combineT"))
                    V.tensor_copy(cstack[0:EXPERTS], ps_acc[0:EXPERTS]).then_inc(mid_dve.sem, 1)
                    m_wait(f, "hi")
                    V.tensor_sub(crem[:], ps_acc[0:EXPERTS], cstack[0:EXPERTS]).then_inc(mid_dve.sem, 1)
                    m_wait(f, "rem")
                    V.tensor_copy(cmid[:], crem[:]).then_inc(mid_dve.sem, 1)
                    m_wait(f, "mid")
                    V.tensor_copy(cstack[QUAD:QUAD + EXPERTS], cmid[:]).then_inc(mid_dve.sem, 1)
                    V.tensor_sub(cstack[2 * QUAD:2 * QUAD + EXPERTS], crem[:], cmid[:]).then_inc(mid_dve.sem, 1)

                def scan(c, g):
                    dve.wait_ge(du_bc, c * GROUPS + g + 1)
                    wait(dve, h_ready, c * GROUPS + g - 1)
                    V.tensor_mul(dbu[:, g % 2], B_bc[:], ps_du[:]).then_inc(dbu_ready, 1)
                    dve.wait_ge(a_ready, c * GROUPS + g + 1)
                    dve.wait_ge(dbu_ready, c * GROUPS + g + 1)
                    wait(dve, hc_ready, c * GROUPS + g + 1 - H_RING)
                    wait(dve, state_saved, c * BLOCKS + g // BLOCK - 1)
                    V.tensor_tensor_scan(h[:, g % H_RING], a[:, g % A_RING], dbu[:, g % 2], state[:, g:g + 1],
                                         ALU.mult, ALU.add).then_inc(h_ready, 1)
                    if g % BLOCK == BLOCK - 1:
                        dve.wait_ge(h_ready, c * GROUPS + g + 1)
                        at = (g + 1 - BLOCK) % H_RING
                        V.tensor_copy(state[:, g + 1 - BLOCK:g + 1], h[:, at:at + BLOCK, TOK - 1]).then_inc(state_saved, 1)

                def gate(c, m):
                    dve.wait_ge(y_added, c * BLOCKS + (m + 1) * NJ)
                    V.scalar_tensor_tensor(yg[:, m], u[:, m], skip_D[:, m:m + 1], ps_y[:], ALU.mult, ALU.add).then_inc(y_read, 1)
                    dve.wait_ge(y_read, c * TILES + m + 1)
                    V.tensor_mul(yg[:, m], yg[:, m], z[:, m]).then_inc(yg_ready, 1)

                def unit(f, e):
                    dve.wait_ge(th_ready, f * UNITS + e + 1)
                    if e >= 2:
                        dve.wait_ge(sc_ready, f * EXPERTS + min(e - 1, EXPERTS))
                        dve.wait_ge(act_ready, f * UNITS + e - 1)
                    V.scalar_tensor_tensor(sg[:, e % 2], th[:, e % 2], 1.0, ps_g[:], ALU.add, ALU.mult).then_inc(sg_ready, 1)

                def unit_up(f, e):
                    dve.wait_ge(u_ps, f * UNITS + e + 1)
                    if e >= 2:
                        dve.wait_ge(down, f * UNITS + e - 1)
                    if e < EXPERTS:
                        dve.wait_ge(sc_ready, f * EXPERTS + e + 1)
                        V.tensor_mul(act_o[:, e % 2], sc[:, e % 2], ps_u[:]).then_inc(act_ready, 1)
                    else:
                        dve.wait_ge(sg_ready, f * UNITS + e + 1)
                        V.scalar_tensor_tensor(act_o[:, e % 2], sg[:, e % 2], 0.5, ps_u[:], ALU.mult, ALU.mult).then_inc(act_ready, 1)

                def finish(f):
                    dve.wait_ge(down, (f + 1) * UNITS)
                    V.scalar_tensor_tensor(x2[:], ps_acc[:], gb, x2[:], ALU.mult, ALU.add).then_inc(out_ready, 1)

                def iteration(c, scan_=True, ffn=True):
                    f = c - 1
                    if scan_:
                        front_a(c)
                    if ffn:
                        mid_a(f)
                    if scan_:
                        front_b(c)
                    if ffn:
                        mid_b(f)
                        mid_c(f)
                    if scan_:
                        front_c(c)
                    if ffn:
                        mid_d(f)
                        mid_e(f)
                    if scan_:
                        front_d(c)
                        for g in range(GROUPS):
                            scan(c, g)
                            if ffn:
                                if g and unit_at(g - 1) is not None:
                                    unit_up(f, unit_at(g - 1))
                                if unit_at(g) is not None:
                                    unit(f, unit_at(g))
                            if g == GROUPS // TILES + 2 * BLOCK - 1:
                                gate(c, 0)
                        if ffn and unit_at(GROUPS - 1) is not None:
                            unit_up(f, unit_at(GROUPS - 1))
                        gate(c, 1)
                    elif ffn:
                        for e in range(UNITS):
                            unit(f, e)
                            unit_up(f, e)
                    if ffn:
                        finish(f)

                setup()
                iteration(0, ffn=False)
                with dve.Fori(1, CHUNKS) as c:
                    iteration(c)
                iteration(CHUNKS, scan_=False)


FIRST_UNIT = 4


def unit_at(g):
    n = GROUPS - FIRST_UNIT
    if g < FIRST_UNIT:
        return None
    k = g - FIRST_UNIT
    now, before = (k + 1) * UNITS // n, k * UNITS // n
    return before if now > before else None


def program(nc, args):
    from contextlib import ExitStack

    import concourse.bass as bass
    from concourse import mybir

    build(nc, mybir, ExitStack, {**args, "ds": bass.ds})


def kernel(**inputs):
    import ml_dtypes
    import numpy as np
    import concourse.bacc as bacc
    from concourse import mybir
    from concourse.bass_utils import run_bass_kernel_spmd

    w = {k.replace("L0_", ""): np.asarray(v) for k, v in inputs.items()}

    def tiles(m):
        return m.reshape(-1, P, m.shape[-1]).transpose(1, 0, 2)

    part = np.arange(P)
    f32 = np.float32
    xp = w["attn_x_proj_w"]
    pad = np.zeros((P, DI), f32)
    pad[:RANK] = xp[:RANK]
    dtp = np.zeros((P, DI), f32)
    dtp[:RANK] = w["attn_dt_proj_w"].T
    g = np.arange(GROUPS)
    first = P * (g // (GROUPS // TILES)) + QUAD * (g % NQ) + CH * (g // NQ % NJ)
    A_log = w["attn_A_log"][first[None, :] + (part % CH)[:, None], (part // CH)[:, None]]
    pick = np.zeros((P, NJ, P), f32)
    gather = np.zeros((P, NJ, QUAD), f32)
    for j in range(NJ):
        for k in range(PARTS):
            pick[QUAD * k + CH * j + part % CH, j, part] = 1
        gather[part, j, CH * j + part % CH] = 1
    pick_e = np.zeros((P, EXPERTS, P), f32)
    for e in range(EXPERTS):
        for k in range(PARTS):
            pick_e[QUAD * k + e, e] = 1
    i = np.arange(EXPERTS)
    tri = np.broadcast_to((i[None, :] < i[:, None]).astype(f32), (P, EXPERTS, EXPERTS))

    def units(e, sh):
        return np.concatenate([e, sh], axis=1)

    halves = lambda m: m.reshape(P, SHARED, P)
    small = np.concatenate([tiles(w["attn_conv_w"][:, 0]).reshape(P, -1)] +
                           [tiles(w[k][:, None]).reshape(P, -1) for k in ("attn_conv_b", "attn_dt_proj_b", "attn_D")], axis=1)
    arrays = {
        "x": w["attn_x"][0].T,
        "w_in": w["attn_in_proj_w"].T,
        "w_dt": tiles(pad.T),
        "w_B": tiles(xp[RANK + part // CH].T),
        "w_C": tiles(xp[RANK + NS + part // CH].T),
        "w_dtp": dtp,
        "w_out": tiles(w["attn_out_proj_w"].T),
        "small": small,
        "A_log": A_log,
        "w_router": w["ffn_router_w"].T,
        "r_bias": np.broadcast_to(w["ffn_bias"], (P, EXPERTS)),
        "w_gate": units(w["ffn_gate_w"].transpose(1, 0, 2), halves(w["ffn_sh_gate_w"])),
        "w_up": units(w["ffn_up_w"].transpose(1, 0, 2), halves(w["ffn_sh_up_w"])),
        "w_down": units(w["ffn_down_w"].transpose(1, 0, 2), w["ffn_sh_down_w"].reshape(SHARED, P, DM).transpose(1, 0, 2)),
        "ones": np.full((P, P), 1.0 / DM, f32),
        "ident": np.eye(P, dtype=f32),
        "tri": tri,
        "tri_g": tri[:, :NG, :NG],
        "pick": pick.astype(ml_dtypes.bfloat16),
        "gather": gather,
        "pick_e": pick_e.astype(ml_dtypes.bfloat16),
        "w_mod": w["wmod"].reshape(P, 2, 3 * P),
        "cvec": w["c"].reshape(P, 1),
    }
    nc = bacc.Bacc("TRN2", target_bir_lowering=False, num_devices=1)
    feed, args = {}, {}
    for name, a in arrays.items():
        a = np.ascontiguousarray(a)
        feed[f"in_{name}"] = a
        args[name] = nc.dram_tensor(f"in_{name}", a.shape, mybir.dt.from_np(a.dtype), kind="ExternalInput").ap()
    args["out"] = nc.dram_tensor("out_T", (DM, SEQ), mybir.dt.float32, kind="ExternalOutput").ap()
    program(nc, args)
    r = run_bass_kernel_spmd(nc, [feed], core_ids=[0])
    return np.ascontiguousarray(r.results[0]["out_T"].T)[None]
```

```python
P = 128
SEQ, DM = 2048, 128
TOK = 512
CHUNKS = SEQ // TOK
DI, NS, RANK, TAPS = 256, 16, 64, 4
TILES = DI // P
CH = P // NS
GROUPS = DI // CH
QUAD = 32
PARTS = 3
ROWS = PARTS * QUAD
NQ = P // QUAD
NJ = QUAD // CH
BLOCK = NQ
BLOCKS = GROUPS // BLOCK
EXPERTS, SHARED, NG, TOPG, TOPK = 16, 2, 4, 2, 4
EPG = EXPERTS // NG
UNITS = EXPERTS + SHARED
SUB = TOK // P
EPS = 1e-5
ROUTE_SCALE = 2.5
A_RING, H_RING, HC_RING = 8, 8, 8

FRONT_PE = ["mean", "var", "in0", "in1", "dt", "pre0", "pre1", "B", "C"]
FRONT_ACT = ["sq", "lnv", "rstd", "halo", "xs0", "tap0", "xs1", "tap1", "ut0", "ut1", "dt",
             "abs0", "relu0", "abs1", "relu1", "exp0", "one0", "ln0", "exp1", "one1", "ln1",
             "hi_delta", "hi_du", "mid_delta", "mid_du", "B", "C"]
FRONT_DVE = ["xc", "xn", "h", "conv01", "conv02", "conv03", "conv11", "conv12", "conv13", "u0", "u1", "res0", "res1"]
FRONT_POOL = ["log0", "delta0", "log1", "delta1", "du", "rem_delta", "rem_du", "lo_delta", "lo_du"]
GATE_PE = ["in2", "in3"]
GATE_ACT = ["tanh0", "tanh1", "skip0", "skip1"]
GATE_DVE = ["z0", "z1"]
MID_PE = ["out", "mean", "var", "logits", "combineT"]
MID_ACT = ["sq", "lnv", "rstd", "explog"]
MID_DVE = ["x2", "xc", "xn", "h", "combine", "hi", "rem", "mid", "midrow", "lo"]
ROUTER_FIRST = 19
ROUTER_STEPS = ROUTER_FIRST + 5 * SUB + 5

LEAD = 4
UNIT_SLOTS = [8, 9] + [14 + k for k in range(EXPERTS)] + [30, 31, 31]


class Steps:

    def __init__(self, sem, names):
        self.sem, self.names = sem, names

    def done(self, chunk, name):
        return chunk * len(self.names) + (self.names.index(name) + 1)


def wait(engine, sem, value):
    if isinstance(value, int) and value <= 0:
        return
    engine.wait_ge(sem, value)


def build(nc, mybir, ExitStack, t):
    F32, BF16 = mybir.dt.float32, mybir.dt.bfloat16
    ALU, ACT, AX = mybir.AluOpType, mybir.ActivationFunctionType, mybir.AxisListType
    ctx = ExitStack()
    with ctx:
        def sb(name, shape, dt=F32):
            return ctx.enter_context(nc.sbuf_tensor(name, shape, dt))

        def sem(name):
            return ctx.enter_context(nc.semaphore(name))

        x = sb("x", [P, SEQ])
        w_in = sb("w_in", [P, 2 * DI])
        w_dt = sb("w_dt", [P, TILES, P])
        w_B = sb("w_B", [P, TILES, P])
        w_C = sb("w_C", [P, TILES, P])
        w_dtp = sb("w_dtp", [P, DI])
        w_out = sb("w_out", [P, TILES, P])
        small = sb("small", [P, TILES * (TAPS + 3)])
        conv_w = small[:, 0:TILES * TAPS].rearrange("p (m k) -> p m k", k=TAPS)
        conv_b = small[:, TILES * TAPS:TILES * (TAPS + 1)]
        dt_b = small[:, TILES * (TAPS + 1):TILES * (TAPS + 2)]
        skip_D = small[:, TILES * (TAPS + 2):]
        conv_wh = sb("conv_wh", [P, TILES, TAPS])
        conv_bh = sb("conv_bh", [P, TILES])
        A_log = sb("A_log", [P, GROUPS])
        A_neg = sb("A_neg", [P, GROUPS])
        w_router = sb("w_router", [P, EXPERTS])
        r_bias = sb("r_bias", [P, EXPERTS])
        w_gate = sb("w_gate", [P, UNITS, P])
        w_up = sb("w_up", [P, UNITS, P])
        w_down = sb("w_down", [P, UNITS, P])
        ones = sb("ones", [P, P])
        ident = sb("ident", [P, P])
        tri = sb("tri", [P, EXPERTS, EXPERTS])
        tri_g = sb("tri_g", [P, NG, NG])
        pick = sb("pick", [P, NJ, P], BF16)
        gather = sb("gather", [P, NJ, QUAD])
        pick_e = sb("pick_e", [P, EXPERTS, P], BF16)
        eps = sb("eps", [P, 1])
        cvec = sb("cvec", [P, 4])
        mod = sb("mod", [P, 6])
        scale1 = sb("scale1", [P, 8])
        xc1 = sb("xc1", [P, TOK])
        sq1 = sb("sq1", [P, TOK])
        h1 = sb("h1", [P, TOK])
        xs = sb("xs", [P, TILES, TOK + TAPS - 1])
        u = sb("u", [P, TILES, TOK])
        z = sb("z", [P, TILES, TOK])
        dt = sb("dt", [P, TOK])
        B_bc = sb("B_bc", [P, TOK])
        C_bc = sb("C_bc", [P, TOK])
        cv = sb("cv", [P, TILES, TOK])
        sp = sb("sp", [P, TILES, 4, TOK])
        parts = sb("parts", [P, 2, PARTS, TILES, TOK], BF16)
        stack = sb("stack", [P, 2, NQ, TILES, TOK], BF16)
        a = sb("a", [P, A_RING, TOK])
        dbu = sb("dbu", [P, 2, TOK])
        h = sb("h", [P, H_RING, TOK])
        hc = sb("hc", [P, HC_RING, TOK])
        state = sb("state", [P, GROUPS])
        yg = sb("yg", [P, TILES, TOK])
        rem, du, delta = [sp[:, :, k] for k in range(2)], sp[:, :, 2], sp[:, :, 3]
        w_mod = hc[:, 0:2, 0:3 * P]
        x2 = sb("x2", [P, TOK])
        xc2 = sb("xc2", [P, TOK])
        sq2 = sb("sq2", [P, TOK])
        h2 = sb("h2", [P, TOK])
        out_sb = sb("out_sb", [P, TOK])
        score = sb("score", [P, SUB, EXPERTS])
        sel = sb("sel", [P, SUB, EXPERTS])
        comb = sb("comb", [P, SUB, EXPERTS])
        rt = sb("rt", [P, 8, SUB * EXPERTS])
        gpair = sb("gpair", [P, 2, SUB * NG * NG])
        pair = sb("pair", [P, 2, EXPERTS, EXPERTS])
        cstack = sb("cstack", [P, TOK], BF16)
        crem = pair[0:EXPERTS, :, :, :].rearrange("p a b c -> p (a b c)")
        cmid = sb("cmid", [EXPERTS, TOK], BF16)
        th = sb("th", [P, 2, TOK])
        sg = th
        cb = sb("cb", [P, 2, TOK])
        sc = sb("sc", [P, 2, TOK])
        act_o = sc

        bank = [ctx.enter_context(nc.psum_tensor(f"bank{i}", [P, TOK], F32)) for i in range(8)]
        ps_delta, ps_front, ps_du, ps_y, ps_acc, ps_g, ps_u, ps_cb = bank

        front_pe = Steps(sem("front_pe"), FRONT_PE)
        front_act = Steps(sem("front_act"), FRONT_ACT)
        front_dve = Steps(sem("front_dve"), FRONT_DVE)
        front_pool = Steps(sem("front_pool"), FRONT_POOL)
        gate_pe = Steps(sem("gate_pe"), GATE_PE)
        gate_act = Steps(sem("gate_act"), GATE_ACT)
        gate_dve = Steps(sem("gate_dve"), GATE_DVE)
        mid_pe = Steps(sem("mid_pe"), MID_PE)
        mid_act = Steps(sem("mid_act"), MID_ACT)
        mid_dve = Steps(sem("mid_dve"), MID_DVE)
        router = sem("router")
        x_in, w_a, w_b, w_c = sem("x_in"), sem("w_a"), sem("w_b"), sem("w_c")
        setup_dve, setup_act, setup_pe = sem("setup_dve"), sem("setup_act"), sem("setup_pe")
        delta_in, du_in = sem("delta_in"), sem("du_in")
        delta_bc, du_bc, a_ready, dbu_ready = sem("delta_bc"), sem("du_bc"), sem("a_ready"), sem("dbu_ready")
        h_ready, state_saved, hc_ready, y_added = sem("h_ready"), sem("state_saved"), sem("hc_ready"), sem("y_added")
        y_read, yg_ready = sem("y_read"), sem("yg_ready")
        cb_ps, g_ps, u_ps, down = sem("cb_ps"), sem("g_ps"), sem("u_ps"), sem("down")
        cb_ready, th_ready, sg_ready, sc_ready, act_ready = sem("cb_ready"), sem("th_ready"), sem("sg_ready"), sem("sc_ready"), sem("act_ready")
        out_ready, out_done = sem("out_ready"), sem("out_done")
        SETUP_DVE = 16

        def cols(c):
            return slice(c * TOK, (c + 1) * TOK)

        def xcols(c):
            return x[:, bass_ds(c * TOK, TOK)]

        bass_ds = t["ds"]
        BIG_LOADS = [(w_gate, "w_gate"), (w_up, "w_up"), (w_down, "w_down")]
        FRONT_LOADS = [(w_in, "w_in"), (w_dt, "w_dt"), (w_B, "w_B"), (w_C, "w_C"), (w_dtp, "w_dtp"), (ones, "ones"),
                       (small, "small"), (A_log, "A_log"), (pick, "pick"), (gather, "gather"), (w_mod, "w_mod"),
                       (cvec[:, 0:1], "cvec")]
        MID_LOADS = [(w_out, "w_out"), (w_router, "w_router"), (r_bias, "r_bias"), (ident, "ident"), (tri, "tri"),
                     (tri_g, "tri_g"), (pick_e, "pick_e")]

        with nc.Block() as block:

            @block.sync
            def _(sp_eng):
                sp_eng.dma_start(x[:, 0:TOK], t["x"][:, 0:TOK]).then_inc(x_in, 16)
                for dst, name in FRONT_LOADS:
                    sp_eng.dma_start(dst[:], t[name]).then_inc(w_a, 16)
                sp_eng.wait_ge(x_in, 16)
                sp_eng.dma_start(x[:, TOK:], t["x"][:, TOK:]).then_inc(x_in, 16)
                for dst, name in MID_LOADS:
                    sp_eng.dma_start(dst[:], t[name]).then_inc(w_b, 16)
                for dst, name in BIG_LOADS:
                    sp_eng.dma_start(dst[:], t[name]).then_inc(w_c, 16)

                def restack(n):
                    ready = [[(front_act, "hi_delta"), (front_act, "mid_delta"), (front_pool, "lo_delta")],
                             [(front_act, "hi_du"), (front_act, "mid_du"), (front_pool, "lo_du")]]
                    wait(sp_eng, delta_bc, n * GROUPS)
                    for kind, arrived in enumerate([delta_in, du_in]):
                        for part in range(PARTS):
                            stage, step = ready[kind][part]
                            sp_eng.wait_ge(stage.sem, stage.done(n, step))
                            if kind == 1 and part == 0:
                                wait(sp_eng, du_bc, n * GROUPS)
                            for q in range(NQ):
                                sp_eng.dma_start(stack[QUAD * part:QUAD * (part + 1), kind, q],
                                                 parts[QUAD * q:QUAD * (q + 1), kind, part]).then_inc(arrived, 16)

                def store(f):
                    sp_eng.wait_ge(out_ready, f + 2)
                    sp_eng.dma_start(t["out"][:, bass_ds(f * TOK, TOK)], out_sb[:]).then_inc(out_done, 16)

                restack(0)
                restack(1)
                with sp_eng.Fori(1, CHUNKS - 1) as c:
                    restack(c + 1)
                    store(c - 1)
                store(CHUNKS - 2)
                store(CHUNKS - 1)
                sp_eng.wait_ge(out_done, 16 + 16 * CHUNKS)

            @block.tensor
            def _(pe):
                def mm(out, lhsT, rhs, start=True, stop=True):
                    return nc.tensor.matmul(out, lhsT, rhs, start=start, stop=stop)

                def front_mean(n):
                    wait(pe, gate_dve.sem, gate_dve.done(n - 1, "z1"))
                    if isinstance(n, int):
                        pe.wait_ge(x_in, 16 if n == 0 else 32)
                    mm(ps_front[:], ones[:], xcols(n)).then_inc(front_pe.sem, 1)

                def front_var(n):
                    pe.wait_ge(front_dve.sem, front_dve.done(n, "xc"))
                    pe.wait_ge(front_act.sem, front_act.done(n, "sq"))
                    mm(ps_front[:], ones[:], sq1[:]).then_inc(front_pe.sem, 1)

                def front_in(n, m):
                    if m == 0:
                        pe.wait_ge(front_dve.sem, front_dve.done(n, "h"))
                    else:
                        pe.wait_ge(front_act.sem, front_act.done(n, "xs0"))
                    mm(ps_front[:], w_in[:, m * P:(m + 1) * P], h1[:]).then_inc(front_pe.sem, 1)

                def from_u(w):
                    for m in range(TILES):
                        last = mm(ps_front[:], w[:, m], u[:, m], start=m == 0, stop=m == TILES - 1)
                    last.then_inc(front_pe.sem, 1)

                def front_dt(n):
                    pe.wait_ge(front_act.sem, front_act.done(n, "xs1"))
                    pe.wait_ge(front_dve.sem, front_dve.done(n, "u1"))
                    from_u(w_dt)

                def front_pre(n, m):
                    pe.wait_ge(front_act.sem, front_act.done(n, "relu0" if m else "dt"))
                    mm(ps_front[:], w_dtp[:, m * P:(m + 1) * P], dt[:]).then_inc(front_pe.sem, 1)

                def front_B(n):
                    pe.wait_ge(front_act.sem, front_act.done(n, "relu1"))
                    from_u(w_B)

                def front_C(n):
                    pe.wait_ge(front_act.sem, front_act.done(n, "B"))
                    from_u(w_C)

                def gate_in(c, m):
                    if m == 0:
                        pe.wait_ge(front_act.sem, front_act.done(c, "C"))
                    else:
                        pe.wait_ge(gate_dve.sem, gate_dve.done(c, "z0"))
                    mm(ps_front[:], w_in[:, (TILES + m) * P:(TILES + m + 1) * P], h1[:]).then_inc(gate_pe.sem, 1)

                def mid_out(f):
                    pe.wait_ge(yg_ready, TILES * f + TILES)
                    pe.wait_ge(out_ready, f + 1)
                    for m in range(TILES):
                        last = mm(ps_acc[:], w_out[:, m], yg[:, m], start=m == 0, stop=m == TILES - 1)
                    last.then_inc(mid_pe.sem, 1)

                def mid_mean(f):
                    pe.wait_ge(mid_dve.sem, mid_dve.done(f, "x2"))
                    mm(ps_acc[:], ones[:], x2[:]).then_inc(mid_pe.sem, 1)

                def mid_var(f):
                    pe.wait_ge(mid_act.sem, mid_act.done(f, "sq"))
                    mm(ps_acc[:], ones[:], sq2[:]).then_inc(mid_pe.sem, 1)

                def mid_logits(f):
                    pe.wait_ge(mid_dve.sem, mid_dve.done(f, "h"))
                    for s in range(SUB):
                        last = mm(ps_acc[:, s * EXPERTS:(s + 1) * EXPERTS], h2[:, s * P:(s + 1) * P], w_router[:])
                    last.then_inc(mid_pe.sem, 1)

                def mid_combine(f):
                    pe.wait_ge(mid_dve.sem, mid_dve.done(f, "combine"))
                    for s in range(SUB):
                        last = nc.tensor.transpose(ps_acc[0:EXPERTS, s * P:(s + 1) * P], comb[:, s], ident[:])
                    last.then_inc(mid_pe.sem, 1)

                def tile_of(g):
                    return g // (GROUPS // TILES), g % NQ, g // NQ % NJ

                def broadcast_delta(c, g):
                    tile, q, j = tile_of(g)
                    wait(pe, a_ready, c * GROUPS + g)
                    mm(ps_delta[:], pick[0:ROWS, j], stack[0:ROWS, 0, q, tile]).then_inc(delta_bc, 1)

                def broadcast_du(c, g):
                    tile, q, j = tile_of(g)
                    wait(pe, dbu_ready, c * GROUPS + g)
                    mm(ps_du[:], pick[0:ROWS, j], stack[0:ROWS, 1, q, tile]).then_inc(du_bc, 1)

                def add_states(c, b):
                    j = b % NJ
                    pe.wait_ge(hc_ready, c * GROUPS + BLOCK * (b + 1))
                    if j == 0:
                        wait(pe, y_read, c * TILES + b // NJ)
                    for q in range(NQ):
                        last = mm(ps_y[QUAD * q:QUAD * (q + 1), :], gather[:, j], hc[:, (BLOCK * b + q) % HC_RING],
                                  start=j == 0, stop=j == NJ - 1)
                    last.then_inc(y_added, 1)

                def unit(f, k):
                    if SHARED <= k < UNITS:
                        if k == SHARED:
                            pe.wait_ge(mid_dve.sem, mid_dve.done(f, "lo"))
                        else:
                            pe.wait_ge(cb_ready, f * EXPERTS + k - SHARED)
                        mm(ps_cb[:], pick_e[:, k - SHARED], cstack[:]).then_inc(cb_ps, 1)
                    if k >= 3:
                        pe.wait_ge(act_ready, f * UNITS + k - 2)
                        mm(ps_acc[:], w_down[:, k - 3], act_o[:, (k - 3) % 2], start=k == 3,
                           stop=k == UNITS + 2).then_inc(down, 1)
                    if k < UNITS:
                        if k:
                            pe.wait_ge(sg_ready, f * UNITS + k)
                        mm(ps_g[:], w_gate[:, k], h2[:]).then_inc(g_ps, 1)
                    if 1 <= k <= UNITS:
                        if k >= 2:
                            pe.wait_ge(act_ready, f * UNITS + k - 1)
                        mm(ps_u[:], w_up[:, k - 1], h2[:]).then_inc(u_ps, 1)

                def iteration(c, scan=True, ffn=True, front=True):
                    f, n = c - 1, c + 1
                    if scan:
                        pe.wait_ge(delta_in, 16 * PARTS * NQ * c + 16 * PARTS * NQ)
                        for g in range(LEAD):
                            broadcast_delta(c, g)
                        pe.wait_ge(du_in, 16 * PARTS * NQ * c + 16 * PARTS * NQ)
                        broadcast_du(c, 0)
                    for s in range(GROUPS):
                        if scan:
                            if s + 1 < GROUPS:
                                broadcast_du(c, s + 1)
                            if s + LEAD < GROUPS:
                                broadcast_delta(c, s + LEAD)
                        if s == 0:
                            if ffn:
                                add_states(f, BLOCKS - 1)
                            if scan:
                                front_C(c)
                        if scan:
                            if s == 1:
                                gate_in(c, 0)
                            if s == 3:
                                gate_in(c, 1)
                        if ffn:
                            if s == 2:
                                mid_out(f)
                            if s == 4:
                                mid_mean(f)
                            if s == 6:
                                mid_var(f)
                            if s == 8:
                                mid_logits(f)
                            if s == 12:
                                mid_combine(f)
                        if front:
                            if s == 5:
                                front_mean(n)
                            if s == 7:
                                front_var(n)
                            if s == 9:
                                front_in(n, 0)
                            if s == 10:
                                front_in(n, 1)
                            if s == 18:
                                front_dt(n)
                            if s == 19:
                                front_pre(n, 0)
                            if s == 20:
                                front_pre(n, 1)
                            if s == GROUPS - 2:
                                front_B(n)
                        if ffn:
                            for k in units_at(s):
                                unit(f, k)
                        if scan and s % BLOCK == BLOCK - 1 and s >= 2 * BLOCK - 1:
                            add_states(c, s // BLOCK - 1)

                pe.wait_ge(w_a, 16 * len(FRONT_LOADS))
                pe.wait_ge(setup_dve, 3)
                for k in range(6):
                    last = mm(ps_acc[:, k:k + 1], w_mod[:, k // 3, (k % 3) * P:(k % 3 + 1) * P], cvec[:, 3:4])
                last.then_inc(setup_pe, 1)
                front_mean(0)
                front_var(0)
                front_in(0, 0)
                front_in(0, 1)
                front_dt(0)
                front_pre(0, 0)
                front_pre(0, 1)
                front_B(0)
                iteration(0, ffn=False)
                pe.wait_ge(w_b, 16 * len(MID_LOADS))
                pe.wait_ge(w_c, 16 * len(BIG_LOADS))
                with pe.Fori(1, CHUNKS - 1) as c:
                    iteration(c)
                iteration(CHUNKS - 1, front=False)
                iteration(CHUNKS, scan=False, front=False)

            @block.scalar
            def _(act):
                def ln_exp_set():
                    nc.scalar.preload_act_table_set("natural_log_exp_and_others")

                def exp_tanh_set():
                    nc.scalar.preload_act_table_set("exp_and_others")

                def front_sq(n):
                    act.wait_ge(front_dve.sem, front_dve.done(n, "xc"))
                    nc.scalar.activation(sq1[:], xc1[:], ACT.Square).then_inc(front_act.sem, 1)

                def front_rstd(n):
                    act.wait_ge(front_pe.sem, front_pe.done(n, "var"))
                    nc.scalar.activation(sq1[:], ps_front[:], ACT.Ln, bias=eps[:]).then_inc(front_act.sem, 1)
                    act.wait_ge(front_act.sem, front_act.done(n, "lnv"))
                    nc.scalar.activation(sq1[:], sq1[:], ACT.Exp, scale=-0.5).then_inc(front_act.sem, 1)

                def front_halo(n):
                    wait(act, front_dve.sem, front_dve.done(n - 1, "conv13"))
                    wait(act, front_act.sem, front_act.done(n - 1, "tap1"))
                    nc.scalar.copy(xs[:, :, 0:TAPS - 1], xs[:, :, TOK:]).then_inc(front_act.sem, 1)
                    act.wait_ge(front_act.sem, front_act.done(n, "halo"))

                def front_xs(n, m):
                    act.wait_ge(front_pe.sem, front_pe.done(n, f"in{m}"))
                    nc.scalar.copy(xs[:, m, TAPS - 1:], ps_front[:]).then_inc(front_act.sem, 1)
                    act.wait_ge(front_act.sem, front_act.done(n, f"xs{m}"))
                    nc.scalar.activation(cv[:, m], xs[:, m, 0:TOK], ACT.Identity, scale=conv_wh[:, m, 0:1],
                                         bias=conv_bh[:, m:m + 1]).then_inc(front_act.sem, 1)

                def front_u(n):
                    for m in range(TILES):
                        act.wait_ge(front_dve.sem, front_dve.done(n, f"conv{m}3"))
                        nc.scalar.activation(u[:, m], cv[:, m], ACT.Tanh).then_inc(front_act.sem, 1)

                def front_dt(n):
                    act.wait_ge(front_pe.sem, front_pe.done(n, "dt"))
                    nc.scalar.copy(dt[:], ps_front[:]).then_inc(front_act.sem, 1)

                def front_abs(n, m):
                    if m == 0:
                        wait(act, front_pool.sem, front_pool.done(n - 1, "lo_du"))
                    act.wait_ge(front_pe.sem, front_pe.done(n, f"pre{m}"))
                    nc.scalar.activation(sp[:, m, 0], ps_front[:], ACT.Abs, bias=dt_b[:, m:m + 1]).then_inc(front_act.sem, 1)
                    nc.scalar.activation(sp[:, m, 3], ps_front[:], ACT.Relu, bias=dt_b[:, m:m + 1]).then_inc(front_act.sem, 1)

                def front_softplus(n):
                    for m in range(TILES):
                        v_exp, v_one, v_ln, v_relu = (sp[:, m, k] for k in range(4))
                        act.wait_ge(front_act.sem, front_act.done(n, f"abs{m}"))
                        nc.scalar.activation(v_exp, v_exp, ACT.Exp, scale=-1.0).then_inc(front_act.sem, 1)
                        act.wait_ge(front_act.sem, front_act.done(n, f"exp{m}"))
                        nc.scalar.activation(v_one, v_exp, ACT.Identity, bias=1.0).then_inc(front_act.sem, 1)
                        nc.scalar.activation(v_ln, v_exp, ACT.Ln, bias=1.0).then_inc(front_act.sem, 1)

                def front_high(n):
                    wait(act, delta_in, 16 * PARTS * NQ * n)
                    wait(act, du_in, 16 * PARTS * NQ * n)
                    act.wait_ge(front_pool.sem, front_pool.done(n, "delta1"))
                    nc.scalar.copy(parts[:, 0, 0], delta).then_inc(front_act.sem, 1)
                    act.wait_ge(front_pool.sem, front_pool.done(n, "du"))
                    nc.scalar.copy(parts[:, 1, 0], du).then_inc(front_act.sem, 1)

                def front_middle(n):
                    act.wait_ge(front_pool.sem, front_pool.done(n, "rem_delta"))
                    nc.scalar.copy(parts[:, 0, 1], rem[0]).then_inc(front_act.sem, 1)
                    act.wait_ge(front_pool.sem, front_pool.done(n, "rem_du"))
                    nc.scalar.copy(parts[:, 1, 1], rem[1]).then_inc(front_act.sem, 1)

                def front_B(n):
                    wait(act, dbu_ready, GROUPS * n)
                    act.wait_ge(front_pe.sem, front_pe.done(n, "B"))
                    nc.scalar.copy(B_bc[:], ps_front[:]).then_inc(front_act.sem, 1)

                def front_C(n):
                    wait(act, hc_ready, GROUPS * n)
                    act.wait_ge(front_pe.sem, front_pe.done(n, "C"))
                    nc.scalar.copy(C_bc[:], ps_front[:]).then_inc(front_act.sem, 1)

                def gate_tanh(c, m):
                    wait(act, yg_ready, TILES * c)
                    act.wait_ge(gate_pe.sem, gate_pe.done(c, f"in{m + 2}"))
                    nc.scalar.activation(z[:, m], ps_front[:], ACT.Tanh, scale=0.5).then_inc(gate_act.sem, 1)

                def gate_skip(c):
                    wait(act, mid_pe.sem, mid_pe.done(c - 1, "out"))
                    act.wait_ge(front_dve.sem, front_dve.done(c, "u1"))
                    for m in range(TILES):
                        nc.scalar.activation(yg[:, m], u[:, m], ACT.Copy, scale=skip_D[:, m:m + 1]).then_inc(gate_act.sem, 1)

                def mid_sq(f):
                    act.wait_ge(mid_dve.sem, mid_dve.done(f, "xc"))
                    nc.scalar.activation(sq2[:], xc2[:], ACT.Square).then_inc(mid_act.sem, 1)

                def mid_rstd(f):
                    act.wait_ge(mid_pe.sem, mid_pe.done(f, "var"))
                    nc.scalar.activation(sq2[:], ps_acc[:], ACT.Ln, bias=eps[:]).then_inc(mid_act.sem, 1)
                    act.wait_ge(mid_act.sem, mid_act.done(f, "lnv"))
                    nc.scalar.activation(sq2[:], sq2[:], ACT.Exp, scale=-0.5).then_inc(mid_act.sem, 1)

                def mid_exp(f):
                    act.wait_ge(mid_pe.sem, mid_pe.done(f, "logits"))
                    nc.scalar.activation(rt[:, 0], ps_acc[:, 0:SUB * EXPERTS], ACT.Exp, scale=-1.0).then_inc(mid_act.sem, 1)

                def decay(c, g):
                    act.wait_ge(delta_bc, c * GROUPS + g + 1)
                    wait(act, h_ready, c * GROUPS + g + 1 - A_RING)
                    nc.scalar.activation(a[:, g % A_RING], ps_delta[:], ACT.Exp,
                                         scale=A_neg[:, g:g + 1]).then_inc(a_ready, 1)

                def unit(f, k):
                    if k >= UNITS:
                        return
                    if k >= SHARED:
                        act.wait_ge(cb_ps, f * EXPERTS + k - SHARED + 1)
                        if k >= SHARED + 2:
                            act.wait_ge(sc_ready, f * EXPERTS + k - SHARED - 1)
                        nc.scalar.copy(cb[:, k % 2], ps_cb[:]).then_inc(cb_ready, 1)
                    act.wait_ge(g_ps, f * UNITS + k + 1)
                    if k >= 2:
                        act.wait_ge(act_ready, f * UNITS + k - 1)
                    nc.scalar.activation(th[:, k % 2], ps_g[:], ACT.Tanh, scale=0.5).then_inc(th_ready, 1)

                def iteration(c, scan=True, ffn=True, front=True):
                    f, n = c - 1, c + 1
                    if scan:
                        for g in range(LEAD):
                            decay(c, g)
                    for s in range(GROUPS):
                        if scan and s + LEAD < GROUPS:
                            decay(c, s + LEAD)
                        if s == 0 and scan:
                            front_C(c)
                        if scan:
                            if s == 1:
                                gate_tanh(c, 0)
                            if s == 3:
                                gate_tanh(c, 1)
                            if s == 4:
                                gate_skip(c)
                        if ffn:
                            if s == 5:
                                mid_sq(f)
                            if s == 6:
                                ln_exp_set()
                                mid_rstd(f)
                            if s == 8:
                                mid_exp(f)
                        if front:
                            if s == 6:
                                front_sq(n)
                            if s == 7:
                                ln_exp_set()
                                front_rstd(n)
                                exp_tanh_set()
                            if s == 9:
                                front_halo(n)
                                front_xs(n, 0)
                            if s == 10:
                                front_xs(n, 1)
                            if s == 16:
                                front_u(n)
                            if s == 18:
                                front_dt(n)
                            if s == 19:
                                front_abs(n, 0)
                            if s == 20:
                                front_abs(n, 1)
                                ln_exp_set()
                                front_softplus(n)
                                exp_tanh_set()
                            if s == 25:
                                front_high(n)
                            if s == 27:
                                front_middle(n)
                        elif s == 7 and ffn:
                            exp_tanh_set()
                        if ffn:
                            for k in units_at(s):
                                unit(f, k)
                    if front:
                        front_B(n)

                exp_tanh_set()
                act.wait_ge(w_a, 16 * len(FRONT_LOADS))
                nc.scalar.activation(cvec[:, 1:2], cvec[:, 0:1], ACT.Exp, scale=-1.0).then_inc(setup_act, 1)
                nc.scalar.activation(A_neg[:], A_log[:], ACT.Exp).then_inc(setup_act, 1)
                act.wait_ge(setup_act, 2)
                nc.scalar.mul(A_neg[:], A_neg[:], -1.0).then_inc(setup_act, 1)
                act.wait_ge(setup_pe, 1)
                nc.scalar.copy(mod[:], ps_acc[:, 0:6]).then_inc(setup_act, 1)
                act.wait_ge(setup_act, 4)
                act.wait_ge(setup_dve, SETUP_DVE)
                ln_exp_set()
                front_sq(0)
                front_rstd(0)
                front_halo(0)
                front_xs(0, 0)
                front_xs(0, 1)
                exp_tanh_set()
                front_u(0)
                ln_exp_set()
                front_dt(0)
                front_abs(0, 0)
                front_abs(0, 1)
                front_softplus(0)
                front_high(0)
                front_middle(0)
                front_B(0)
                exp_tanh_set()
                iteration(0, ffn=False)
                with act.Fori(1, CHUNKS - 1) as c:
                    exp_tanh_set()
                    iteration(c)
                exp_tanh_set()
                iteration(CHUNKS - 1, front=False)
                iteration(CHUNKS, scan=False, front=False)

            @block.gpsimd
            def _(pool):
                G = nc.gpsimd

                def own(n, step):
                    pool.wait_ge(front_pool.sem, front_pool.done(n, step))

                def front_delta(n, m):
                    v_exp, v_one, v_ln, v_relu = (sp[:, m, k] for k in range(4))
                    pool.wait_ge(front_dve.sem, front_dve.done(n, f"res{m}"))
                    G.tensor_sub(v_ln, v_ln, v_one).then_inc(front_pool.sem, 1)
                    own(n, f"log{m}")
                    G.tensor_add(delta[:, m], v_ln, v_relu).then_inc(front_pool.sem, 1)

                def front_du(n):
                    own(n, "delta1")
                    G.tensor_mul(du, delta, u[:]).then_inc(front_pool.sem, 1)

                def front_rem(n):
                    for kind, (of, name) in enumerate(((delta, "hi_delta"), (du, "hi_du"))):
                        pool.wait_ge(front_act.sem, front_act.done(n, name))
                        G.tensor_sub(rem[kind], of, parts[:, kind, 0]).then_inc(front_pool.sem, 1)

                def front_low(n):
                    for kind, name in enumerate(("mid_delta", "mid_du")):
                        pool.wait_ge(front_act.sem, front_act.done(n, name))
                        G.tensor_sub(parts[:, kind, 2], rem[kind], parts[:, kind, 1]).then_inc(front_pool.sem, 1)

                def times_C(c, g):
                    pool.wait_ge(h_ready, c * GROUPS + g + 1)
                    wait(pool, y_added, c * BLOCKS + g // BLOCK - 1)
                    G.tensor_mul(hc[:, g % HC_RING], h[:, g % H_RING], C_bc[:]).then_inc(hc_ready, 1)

                def unit(f, k):
                    if not SHARED <= k < UNITS:
                        return
                    pool.wait_ge(sg_ready, f * UNITS + k + 1)
                    pool.wait_ge(cb_ready, f * EXPERTS + k - SHARED + 1)
                    pool.wait_ge(down, f * UNITS + k - 1)
                    G.tensor_mul(sc[:, k % 2], sg[:, k % 2], cb[:, k % 2]).then_inc(sc_ready, 1)

                def iteration(c, scan=True, ffn=True, front=True):
                    f, n = c - 1, c + 1
                    if scan:
                        pool.wait_ge(front_act.sem, front_act.done(c, "C"))
                    for s in range(GROUPS):
                        if scan:
                            times_C(c, s)
                        if front:
                            if s == 22:
                                front_delta(n, 0)
                            if s == 23:
                                front_delta(n, 1)
                            if s == 24:
                                front_du(n)
                            if s == 26:
                                front_rem(n)
                            if s == 28:
                                front_low(n)
                        if ffn:
                            for k in units_at(s):
                                unit(f, k)

                front_delta(0, 0)
                front_delta(0, 1)
                front_du(0)
                front_rem(0)
                front_low(0)
                iteration(0, ffn=False)
                with pool.Fori(1, CHUNKS - 1) as c:
                    iteration(c)
                iteration(CHUNKS - 1, front=False)
                iteration(CHUNKS, scan=False, front=False)

            @block.vector
            def _(dve):
                V = nc.vector
                one_ca, one_cb, ga_half, gb = (scale1[:, k:k + 1] for k in range(4))
                sa, sb_ = mod[:, 0:1], mod[:, 3:4]

                def setup():
                    n = [0]

                    def link(ins):
                        n[0] += 1
                        ins.then_inc(setup_dve, 1)
                        dve.wait_ge(setup_dve, n[0])

                    dve.wait_ge(setup_act, 1)
                    link(V.tensor_scalar(cvec[:, 2:3], cvec[:, 1:2], 1.0, None, ALU.add))
                    link(V.reciprocal(cvec[:, 1:2], cvec[:, 2:3]))
                    link(V.tensor_mul(cvec[:, 3:4], cvec[:, 0:1], cvec[:, 1:2]))
                    V.memset(eps[:], EPS)
                    V.memset(xs[:], 0.0)
                    V.memset(cstack[:], 0.0)
                    link(V.memset(state[:], 0.0))
                    link(V.tensor_scalar(conv_wh[:], conv_w, 0.5, None, ALU.mult))
                    link(V.tensor_scalar(conv_bh[:], conv_b, 0.5, None, ALU.mult))
                    dve.wait_ge(setup_act, 4)
                    link(V.tensor_scalar(one_ca, mod[:, 1:2], 1.0, None, ALU.add))
                    link(V.tensor_scalar(one_cb, mod[:, 4:5], 1.0, None, ALU.add))
                    for dst, k, sign in ((ga_half, 2, 1.0), (gb, 5, 2.0)):
                        link(V.tensor_scalar(scale1[:, 4:5], mod[:, k:k + 1], 0.0, sign, ALU.is_ge, ALU.mult))
                        link(V.scalar_tensor_tensor(scale1[:, 7:8], mod[:, k:k + 1], -1.0, mod[:, k:k + 1], ALU.mult, ALU.max))
                        V.tensor_scalar(scale1[:, 5:6], scale1[:, 7:8], 0.25, None, ALU.max)
                        link(V.tensor_scalar(scale1[:, 6:7], scale1[:, 4:5], sign / 2, None, ALU.subtract))
                        if k == 2:
                            link(V.tensor_mul(dst, scale1[:, 6:7], scale1[:, 5:6]))
                        else:
                            V.tensor_mul(dst, scale1[:, 6:7], scale1[:, 5:6]).then_inc(setup_dve, 1)
                    assert n[0] == SETUP_DVE - 1, n
                    dve.wait_ge(setup_dve, SETUP_DVE)
                    dve.sem_inc(out_ready, 1)
                    dve.sem_inc(out_done, 16)

                def f_wait(n, step):
                    dve.wait_ge(front_dve.sem, front_dve.done(n, step))

                def front_xc(n):
                    dve.wait_ge(front_pe.sem, front_pe.done(n, "mean"))
                    V.tensor_sub(xc1[:], xcols(n), ps_front[:]).then_inc(front_dve.sem, 1)

                def front_h(n):
                    dve.wait_ge(front_act.sem, front_act.done(n, "rstd"))
                    V.tensor_mul(xc1[:], xc1[:], sq1[:]).then_inc(front_dve.sem, 1)
                    f_wait(n, "xn")
                    V.tensor_scalar(h1[:], xc1[:], one_ca, sa, ALU.mult, ALU.add).then_inc(front_dve.sem, 1)

                def front_conv(n, m):
                    dve.wait_ge(front_act.sem, front_act.done(n, f"tap{m}"))
                    for k in range(1, TAPS):
                        if k > 1:
                            f_wait(n, f"conv{m}{k - 1}")
                        V.scalar_tensor_tensor(cv[:, m], xs[:, m, k:k + TOK], conv_wh[:, m, k:k + 1], cv[:, m],
                                               ALU.mult, ALU.add).then_inc(front_dve.sem, 1)

                def front_u(n):
                    for m in range(TILES):
                        dve.wait_ge(front_act.sem, front_act.done(n, f"ut{m}"))
                        V.scalar_tensor_tensor(u[:, m], u[:, m], 1.0, cv[:, m], ALU.add, ALU.mult).then_inc(front_dve.sem, 1)

                def front_res(n):
                    for m in range(TILES):
                        v_exp, v_one = sp[:, m, 0], sp[:, m, 1]
                        dve.wait_ge(front_act.sem, front_act.done(n, f"ln{m}"))
                        V.scalar_tensor_tensor(v_one, v_one, 1.0, v_exp, ALU.subtract, ALU.subtract).then_inc(front_dve.sem, 1)

                def gate_z(c, m):
                    dve.wait_ge(gate_act.sem, gate_act.done(c, f"tanh{m}"))
                    V.scalar_tensor_tensor(z[:, m], z[:, m], 1.0, ps_front[:], ALU.add, ALU.mult).then_inc(gate_dve.sem, 1)

                def gate(c, m):
                    dve.wait_ge(y_added, c * BLOCKS + (m + 1) * NJ)
                    dve.wait_ge(gate_act.sem, gate_act.done(c, f"skip{m}"))
                    V.tensor_add(yg[:, m], yg[:, m], ps_y[:]).then_inc(y_read, 1)
                    dve.wait_ge(y_read, c * TILES + m + 1)
                    V.tensor_mul(yg[:, m], yg[:, m], z[:, m]).then_inc(yg_ready, 1)

                def m_wait(f, step):
                    dve.wait_ge(mid_dve.sem, mid_dve.done(f, step))

                def mid_x2(f):
                    dve.wait_ge(mid_pe.sem, mid_pe.done(f, "out"))
                    V.scalar_tensor_tensor(x2[:], ps_acc[:], ga_half, xcols(f), ALU.mult, ALU.add).then_inc(mid_dve.sem, 1)

                def mid_xc(f):
                    dve.wait_ge(mid_pe.sem, mid_pe.done(f, "mean"))
                    m_wait(f, "x2")
                    V.tensor_sub(xc2[:], x2[:], ps_acc[:]).then_inc(mid_dve.sem, 1)

                def mid_h(f):
                    dve.wait_ge(mid_act.sem, mid_act.done(f, "rstd"))
                    V.tensor_mul(xc2[:], xc2[:], sq2[:]).then_inc(mid_dve.sem, 1)
                    m_wait(f, "xn")
                    V.tensor_scalar(h2[:], xc2[:], one_cb, sb_, ALU.mult, ALU.add).then_inc(mid_dve.sem, 1)

                def route(f, half):
                    n = [0 if half == 0 else ROUTER_FIRST]

                    def step(ins):
                        n[0] += 1
                        ins.then_inc(router, 1)

                    def link(ins):
                        step(ins)
                        dve.wait_ge(router, f * ROUTER_STEPS + n[0])

                    def by_expert(k):
                        return rt[:, k].rearrange("p (s e) -> p s e", e=EXPERTS)

                    SG = SUB * NG
                    den, biased, masked, rank = (by_expert(k) for k in range(4))
                    if half == 0:
                        dve.wait_ge(mid_act.sem, mid_act.done(f, "explog"))
                        link(V.tensor_scalar(den, den, 1.0, None, ALU.add))
                        link(V.reciprocal(score[:], den))
                        link(V.tensor_tensor(biased, score[:], r_bias[:, :].unsqueeze(1).broadcast_to([P, SUB, EXPERTS]), ALU.add))
                        four = rt[:, 1].rearrange("p (g b a) -> p g b a", a=2, b=2)
                        hi2 = rt[:, 5, 0:2 * SG].rearrange("p (g b) -> p g b", b=2)
                        lo2 = rt[:, 6, 0:2 * SG].rearrange("p (g b) -> p g b", b=2)
                        top1, mid1, low1, gs = (rt[:, 7, k * SG:(k + 1) * SG] for k in range(4))
                        step(V.tensor_tensor(hi2, four[:, :, :, 0], four[:, :, :, 1], ALU.max))
                        link(V.tensor_tensor(lo2, four[:, :, :, 0], four[:, :, :, 1], ALU.min))
                        step(V.tensor_tensor(top1, hi2[:, :, 0], hi2[:, :, 1], ALU.max))
                        step(V.tensor_tensor(mid1, hi2[:, :, 0], hi2[:, :, 1], ALU.min))
                        link(V.tensor_tensor(low1, lo2[:, :, 0], lo2[:, :, 1], ALU.max))
                        link(V.tensor_tensor(mid1, mid1, low1, ALU.max))
                        link(V.tensor_tensor(gs, top1, mid1, ALU.add))
                        gs3 = gs.rearrange("p (s g) -> p s g", g=NG)
                        gj = gs3.unsqueeze(2).broadcast_to([P, SUB, NG, NG])
                        gi = gs3.unsqueeze(3).broadcast_to([P, SUB, NG, NG])
                        gt4, eq4 = (gpair[:, k].rearrange("p (s i j) -> p s i j", i=NG, j=NG) for k in range(2))
                        step(V.tensor_tensor(gt4, gj, gi, ALU.is_gt))
                        link(V.tensor_tensor(eq4, gj, gi, ALU.is_equal))
                        link(V.tensor_tensor(eq4, eq4, tri_g[:, :, :].unsqueeze(1).broadcast_to([P, SUB, NG, NG]), ALU.mult))
                        link(V.tensor_tensor(gt4, gt4, eq4, ALU.add))
                        grank, gm1 = rt[:, 5, 0:SG], rt[:, 6, 0:SG]
                        link(V.tensor_reduce(grank, gpair[:, 0].rearrange("p (q j) -> p q j", j=NG), AX.X, ALU.add))
                        link(V.tensor_scalar(grank, grank, float(TOPG), None, ALU.is_lt))
                        s4 = rt[:, 1].rearrange("p (q e) -> p q e", e=EPG)
                        m4 = rt[:, 2].rearrange("p (q e) -> p q e", e=EPG)
                        step(V.tensor_tensor(m4, s4, grank.unsqueeze(2).broadcast_to([P, SG, EPG]), ALU.mult))
                        link(V.tensor_scalar(gm1, grank, 1.0, None, ALU.subtract))
                        link(V.tensor_tensor(m4, m4, gm1.unsqueeze(2).broadcast_to([P, SG, EPG]), ALU.add))
                        assert n[0] == ROUTER_FIRST, n
                        return
                    for s in range(SUB):
                        ej = masked[:, s].unsqueeze(1).broadcast_to([P, EXPERTS, EXPERTS])
                        ei = masked[:, s].unsqueeze(2).broadcast_to([P, EXPERTS, EXPERTS])
                        step(V.tensor_tensor(pair[:, 0], ej, ei, ALU.is_gt))
                        link(V.tensor_tensor(pair[:, 1], ej, ei, ALU.is_equal))
                        link(V.tensor_tensor(pair[:, 1], pair[:, 1], tri[:], ALU.mult))
                        link(V.tensor_tensor(pair[:, 0], pair[:, 0], pair[:, 1], ALU.add))
                        link(V.tensor_reduce(rank[:, s], pair[:, 0], AX.X, ALU.add))
                    link(V.tensor_scalar(sel[:], rank, float(TOPK), None, ALU.is_lt))
                    link(V.tensor_tensor(sel[:], sel[:], score[:], ALU.mult))
                    total, inverse = rt[:, 6, 0:SUB], rt[:, 5, 0:SUB]
                    link(V.tensor_reduce(total, sel[:], AX.X, ALU.add))
                    link(V.tensor_scalar(total, total, 1e-20, None, ALU.add))
                    link(V.reciprocal(inverse, total))
                    assert n[0] == ROUTER_STEPS, n
                    V.scalar_tensor_tensor(comb[:], sel[:], ROUTE_SCALE / 2,
                                           inverse.unsqueeze(2).broadcast_to([P, SUB, EXPERTS]),
                                           ALU.mult, ALU.mult).then_inc(mid_dve.sem, 1)

                def mid_stack(f):
                    dve.wait_ge(mid_pe.sem, mid_pe.done(f, "combineT"))
                    V.tensor_copy(cstack[0:EXPERTS], ps_acc[0:EXPERTS]).then_inc(mid_dve.sem, 1)
                    m_wait(f, "hi")
                    V.tensor_sub(crem[:], ps_acc[0:EXPERTS], cstack[0:EXPERTS]).then_inc(mid_dve.sem, 1)
                    m_wait(f, "rem")
                    V.tensor_copy(cmid[:], crem[:]).then_inc(mid_dve.sem, 1)
                    m_wait(f, "mid")
                    V.tensor_copy(cstack[QUAD:QUAD + EXPERTS], cmid[:]).then_inc(mid_dve.sem, 1)
                    V.tensor_sub(cstack[2 * QUAD:2 * QUAD + EXPERTS], crem[:], cmid[:]).then_inc(mid_dve.sem, 1)

                def scan_group(c, g):
                    dve.wait_ge(du_bc, c * GROUPS + g + 1)
                    if g == 0:
                        dve.wait_ge(front_act.sem, front_act.done(c, "B"))
                    wait(dve, h_ready, c * GROUPS + g - 1)
                    V.tensor_mul(dbu[:, g % 2], B_bc[:], ps_du[:]).then_inc(dbu_ready, 1)
                    dve.wait_ge(a_ready, c * GROUPS + g + 1)
                    dve.wait_ge(dbu_ready, c * GROUPS + g + 1)
                    wait(dve, hc_ready, c * GROUPS + g + 1 - H_RING)
                    wait(dve, state_saved, c * BLOCKS + g // BLOCK - 1)
                    V.tensor_tensor_scan(h[:, g % H_RING], a[:, g % A_RING], dbu[:, g % 2], state[:, g:g + 1],
                                         ALU.mult, ALU.add).then_inc(h_ready, 1)
                    if g % BLOCK == BLOCK - 1:
                        dve.wait_ge(h_ready, c * GROUPS + g + 1)
                        at = (g + 1 - BLOCK) % H_RING
                        V.tensor_copy(state[:, g + 1 - BLOCK:g + 1], h[:, at:at + BLOCK, TOK - 1]).then_inc(state_saved, 1)

                def unit(f, k):
                    if k < UNITS:
                        dve.wait_ge(th_ready, f * UNITS + k + 1)
                        V.scalar_tensor_tensor(sg[:, k % 2], th[:, k % 2], 1.0, ps_g[:], ALU.add, ALU.mult).then_inc(sg_ready, 1)
                    if 1 <= k <= UNITS:
                        e = k - 1
                        dve.wait_ge(u_ps, f * UNITS + e + 1)
                        if e >= 2:
                            dve.wait_ge(down, f * UNITS + e - 1)
                        if e >= SHARED:
                            dve.wait_ge(sc_ready, f * EXPERTS + e - SHARED + 1)
                            V.tensor_mul(act_o[:, e % 2], sc[:, e % 2], ps_u[:]).then_inc(act_ready, 1)
                        else:
                            dve.wait_ge(sg_ready, f * UNITS + e + 1)
                            V.scalar_tensor_tensor(act_o[:, e % 2], sg[:, e % 2], 0.5, ps_u[:], ALU.mult, ALU.mult).then_inc(act_ready, 1)

                def finish(f):
                    dve.wait_ge(down, (f + 1) * UNITS)
                    dve.wait_ge(out_done, 16 * f + 16)
                    V.scalar_tensor_tensor(out_sb[:], ps_acc[:], gb, x2[:], ALU.mult, ALU.add).then_inc(out_ready, 1)

                def iteration(c, scan=True, ffn=True, front=True):
                    f, n = c - 1, c + 1
                    for s in range(GROUPS):
                        if scan:
                            scan_group(c, s)
                        if scan:
                            if s == 2:
                                gate_z(c, 0)
                            if s == 4:
                                gate_z(c, 1)
                            if s == 21:
                                gate(c, 0)
                        if ffn:
                            if s == 1:
                                gate(f, 1)
                            if s == 3:
                                mid_x2(f)
                            if s == 5:
                                mid_xc(f)
                            if s == 7:
                                mid_h(f)
                            if s == 9:
                                route(f, 0)
                            if s == 10:
                                route(f, 1)
                            if s == 13:
                                mid_stack(f)
                            for k in units_at(s - 1):
                                unit(f, k)
                        if front:
                            if s == 6:
                                front_xc(n)
                            if s == 8:
                                front_h(n)
                            if s == 14:
                                front_conv(n, 0)
                            if s == 15:
                                front_conv(n, 1)
                            if s == 17:
                                front_u(n)
                            if s == 22:
                                front_res(n)
                    if ffn:
                        finish(f)

                setup()
                front_xc(0)
                front_h(0)
                front_conv(0, 0)
                front_conv(0, 1)
                front_u(0)
                front_res(0)
                iteration(0, ffn=False)
                with dve.Fori(1, CHUNKS - 1) as c:
                    iteration(c)
                iteration(CHUNKS - 1, front=False)
                iteration(CHUNKS, scan=False, front=False)


def units_at(s):
    return [k for k, at in enumerate(UNIT_SLOTS) if at == s]


def program(nc, args):
    from contextlib import ExitStack

    import concourse.bass as bass
    from concourse import mybir

    build(nc, mybir, ExitStack, {**args, "ds": bass.ds})


def kernel(**inputs):
    import ml_dtypes
    import numpy as np
    import concourse.bacc as bacc
    from concourse import mybir
    from concourse.bass_utils import run_bass_kernel_spmd

    w = {k.replace("L0_", ""): np.asarray(v) for k, v in inputs.items()}

    def tiles(m):
        return m.reshape(-1, P, m.shape[-1]).transpose(1, 0, 2)

    part = np.arange(P)
    f32 = np.float32
    xp = w["attn_x_proj_w"]
    pad = np.zeros((P, DI), f32)
    pad[:RANK] = xp[:RANK]
    dtp = np.zeros((P, DI), f32)
    dtp[:RANK] = w["attn_dt_proj_w"].T
    g = np.arange(GROUPS)
    first = P * (g // (GROUPS // TILES)) + QUAD * (g % NQ) + CH * (g // NQ % NJ)
    A_log = w["attn_A_log"][first[None, :] + (part % CH)[:, None], (part // CH)[:, None]]
    pick = np.zeros((P, NJ, P), f32)
    gather = np.zeros((P, NJ, QUAD), f32)
    for j in range(NJ):
        for k in range(PARTS):
            pick[QUAD * k + CH * j + part % CH, j, part] = 1
        gather[part, j, CH * j + part % CH] = 1
    pick_e = np.zeros((P, EXPERTS, P), f32)
    for e in range(EXPERTS):
        for k in range(PARTS):
            pick_e[QUAD * k + e, e] = 1
    i = np.arange(EXPERTS)
    tri = np.broadcast_to((i[None, :] < i[:, None]).astype(f32), (P, EXPERTS, EXPERTS))

    def units(shared, experts):
        return np.concatenate([shared, experts], axis=1)

    halves = lambda m: m.reshape(P, SHARED, P)
    small = np.concatenate([tiles(w["attn_conv_w"][:, 0]).reshape(P, -1)] +
                           [tiles(w[k][:, None]).reshape(P, -1) for k in ("attn_conv_b", "attn_dt_proj_b", "attn_D")], axis=1)
    arrays = {
        "x": w["attn_x"][0].T,
        "w_in": w["attn_in_proj_w"].T,
        "w_dt": tiles(pad.T),
        "w_B": tiles(xp[RANK + part // CH].T),
        "w_C": tiles(xp[RANK + NS + part // CH].T),
        "w_dtp": dtp,
        "w_out": tiles(w["attn_out_proj_w"].T),
        "small": small,
        "A_log": A_log,
        "w_router": w["ffn_router_w"].T,
        "r_bias": np.broadcast_to(w["ffn_bias"], (P, EXPERTS)),
        "w_gate": units(halves(w["ffn_sh_gate_w"]), w["ffn_gate_w"].transpose(1, 0, 2)),
        "w_up": units(halves(w["ffn_sh_up_w"]), w["ffn_up_w"].transpose(1, 0, 2)),
        "w_down": units(w["ffn_sh_down_w"].reshape(SHARED, P, DM).transpose(1, 0, 2), w["ffn_down_w"].transpose(1, 0, 2)),
        "ones": np.full((P, P), 1.0 / DM, f32),
        "ident": np.eye(P, dtype=f32),
        "tri": tri,
        "tri_g": tri[:, :NG, :NG],
        "pick": pick.astype(ml_dtypes.bfloat16),
        "gather": gather,
        "pick_e": pick_e.astype(ml_dtypes.bfloat16),
        "w_mod": w["wmod"].reshape(P, 2, 3 * P),
        "cvec": w["c"].reshape(P, 1),
    }
    nc = bacc.Bacc("TRN2", target_bir_lowering=False, num_devices=1)
    feed, args = {}, {}
    for name, a in arrays.items():
        a = np.ascontiguousarray(a)
        feed[f"in_{name}"] = a
        args[name] = nc.dram_tensor(f"in_{name}", a.shape, mybir.dt.from_np(a.dtype), kind="ExternalInput").ap()
    args["out"] = nc.dram_tensor("out_T", (DM, SEQ), mybir.dt.float32, kind="ExternalOutput").ap()
    program(nc, args)
    r = run_bass_kernel_spmd(nc, [feed], core_ids=[0])
    return np.ascontiguousarray(r.results[0]["out_T"].T)[None]
```

```python
P = 128
SEQ, DM = 2048, 128
TOK = 512
CHUNKS = SEQ // TOK
DI, NS, RANK, TAPS = 256, 16, 64, 4
TILES = DI // P
CH = P // NS
GROUPS = DI // CH
QUAD = 32
PARTS = 3
ROWS = PARTS * QUAD
NQ = P // QUAD
NJ = QUAD // CH
BLOCK = NQ
BLOCKS = GROUPS // BLOCK
EXPERTS, SHARED, NG, TOPG, TOPK = 16, 2, 4, 2, 4
EPG = EXPERTS // NG
UNITS = EXPERTS + SHARED
SUB = TOK // P
EPS = 1e-5
ROUTE_SCALE = 2.5
A_RING, H_RING, HC_RING = 8, 8, 8

FRONT_PE = ["mean", "var", "in0", "in1", "dt", "pre0", "pre1", "B", "C"]
FRONT_ACT = ["sq", "lnv", "rstd", "halo", "xs0", "tap00", "tap01", "tap02", "tap03", "xs1", "tap10", "tap11", "tap12", "tap13",
             "ut0", "ut1", "dt",
             "abs0", "relu0", "abs1", "relu1", "exp0", "one0", "exp1", "one1", "ln0", "ln1",
             "hi_delta", "hi_du", "mid_delta", "mid_du"]
BC_ACT = ["B", "C"]
FRONT_DVE = ["xc", "xn", "h", "u0", "u1", "res0", "res1",
             "du0", "du1", "rem_delta0", "rem_delta1"]
CONV, DELTA = ["1", "2", "3"], ["log", "delta"]
FRONT_POOL = ["rem_du0", "rem_du1", "lo_delta0", "lo_delta1", "lo_du0", "lo_du1"]
GATE_PE = ["in2", "in3"]
GATE_ACT = ["tanh0", "tanh1", "skip0", "skip1"]
GATE_DVE = ["z0", "z1"]
MID_PE = ["out", "mean", "var", "logits", "combineT"]
MID_ACT = ["sq", "lnv", "rstd", "explog"]
MID_DVE = ["x2", "xc", "xn", "h", "combine", "hi", "rem", "mid", "hi_col", "mid_col", "lo_col", "stack"]
ROUTER_FIRST = 17
ROUTER_STEPS = ROUTER_FIRST + 3 * SUB + 5

LEAD = 4
DIRECT = 8
SLOTS = {
    "PE gate_in0": 1, "PE gate_in1": 3, "PE mean": 5, "PE var": 7, "PE in0": 9, "PE in1": 10, "PE dt": 14,
    "PE pre0": 15, "PE pre1": 16, "PE B": 22,
    "ACT tanh0": 1, "ACT tanh1": 3, "ACT skip": 4, "ACT sq": 6, "ACT rstd": 7, "ACT xs0": 9, "ACT xs1": 10,
    "ACT u": 12, "ACT dt": 14, "ACT abs0": 15, "ACT abs1": 16, "ACT ln": 17, "ACT high": (20, 21),
    "ACT middle": (22, 23),
    "DVE z0": 2, "DVE z1": 4, "DVE xc": 6, "DVE h": 8, "DVE u": 13, "DVE res": 18, "DVE du": 21, "DVE rem": 22,
    "Pool conv": (9, 11), "Pool delta": (17, 18), "Pool rem_du": (21, 22), "Pool lo_delta": (23, 24),
    "Pool lo_du": (25, 26),
}
SLOTS_NO_FFN = {
    "PE gate_in0": 0, "PE gate_in1": 1, "PE mean": 2, "PE var": 4, "PE in0": 6, "PE in1": 7, "PE dt": 13,
    "PE pre0": 14, "PE pre1": 15, "PE B": 20,
    "ACT tanh0": 0, "ACT tanh1": 1, "ACT skip": 2, "ACT sq": 3, "ACT rstd": 4, "ACT xs0": 7, "ACT xs1": 8,
    "ACT u": 11, "ACT dt": 13, "ACT abs0": 14, "ACT abs1": 15, "ACT ln": 16, "ACT high": (20, 21),
    "ACT middle": (22, 24),
    "DVE z0": 1, "DVE z1": 2, "DVE xc": 3, "DVE h": 6, "DVE u": 12, "DVE res": 18, "DVE du": 21, "DVE rem": 22,
    "Pool conv": (7, 8), "Pool delta": (17, 17), "Pool rem_du": (22, 22), "Pool lo_delta": (23, 23),
    "Pool lo_du": (25, 25),
}
UNIT_SLOTS = [8, 10] + [12 + k for k in range(EXPERTS + 3)]


class Steps:

    def __init__(self, sem, names):
        self.sem, self.names = sem, names

    def done(self, chunk, name):
        return chunk * len(self.names) + (self.names.index(name) + 1)


def wait(engine, sem, value):
    if isinstance(value, int) and value <= 0:
        return
    engine.wait_ge(sem, value)


def build(nc, mybir, ExitStack, t):
    F32, BF16 = mybir.dt.float32, mybir.dt.bfloat16
    ALU, ACT, AX = mybir.AluOpType, mybir.ActivationFunctionType, mybir.AxisListType
    ctx = ExitStack()
    with ctx:
        def sb(name, shape, dt=F32):
            return ctx.enter_context(nc.sbuf_tensor(name, shape, dt))

        def sem(name):
            return ctx.enter_context(nc.semaphore(name))

        x = sb("x", [P, SEQ])
        w_in = sb("w_in", [P, 2 * DI])
        w_dt = sb("w_dt", [P, TILES, P])
        w_B = sb("w_B", [P, TILES, P])
        w_C = sb("w_C", [P, TILES, P])
        w_dtp = sb("w_dtp", [P, DI])
        w_out = sb("w_out", [P, TILES, P])
        small = sb("small", [P, TILES * (TAPS + 3)])
        conv_w = small[:, 0:TILES * TAPS].rearrange("p (m k) -> p m k", k=TAPS)
        conv_b = small[:, TILES * TAPS:TILES * (TAPS + 1)]
        dt_b = small[:, TILES * (TAPS + 1):TILES * (TAPS + 2)]
        skip_D = small[:, TILES * (TAPS + 2):]
        conv_wh = sb("conv_wh", [P, TILES, TAPS])
        conv_bh = sb("conv_bh", [P, TILES])
        A_log = sb("A_log", [P, GROUPS])
        A_neg = sb("A_neg", [P, GROUPS])
        w_router = sb("w_router", [P, EXPERTS])
        r_bias = sb("r_bias", [P, EXPERTS])
        w_gate = sb("w_gate", [P, UNITS, P])
        w_up = sb("w_up", [P, UNITS, P])
        w_down = sb("w_down", [P, UNITS, P])
        ones = sb("ones", [P, P])
        ident = sb("ident", [P, P])
        bar = sb("bar", [P, EXPERTS, EXPERTS])
        pick = sb("pick", [P, NJ, P], BF16)
        gather = sb("gather", [P, NJ, QUAD])
        pick_e = sb("pick_e", [P, EXPERTS, P], BF16)
        eps = sb("eps", [P, 1])
        cvec = sb("cvec", [P, 4])
        mod = sb("mod", [P, 6])
        scale1 = sb("scale1", [P, 8])
        xc1 = sb("xc1", [P, TOK])
        sq1 = sb("sq1", [P, TOK])
        h1 = sb("h1", [P, TOK])
        xs = sb("xs", [P, TILES, TOK + TAPS - 1])
        u = sb("u", [P, TILES, TOK])
        z = sb("z", [P, TILES, TOK])
        dt = sb("dt", [P, TOK])
        B_bc = sb("B_bc", [P, TOK])
        C_bc = sb("C_bc", [P, TOK])
        cv = sb("cv", [P, TILES, TOK])
        sp = sb("sp", [P, TILES, 4, TOK])
        parts = sb("parts", [P, 2, PARTS, TILES, TOK], BF16)
        stack = sb("stack", [P, 2, NQ, TILES, TOK], BF16)
        a = sb("a", [P, A_RING, TOK])
        dbu = sb("dbu", [P, 2, TOK])
        h = sb("h", [P, H_RING, TOK])
        hc = sb("hc", [P, HC_RING, TOK])
        state = sb("state", [P, GROUPS])
        yg = sb("yg", [P, TILES, TOK])
        rem, du, delta = [sp[:, :, k] for k in range(2)], sp[:, :, 2], sp[:, :, 3]
        w_mod = hc[:, 0:2, 0:3 * P]
        x2 = sb("x2", [P, TOK])
        xc2 = sb("xc2", [P, TOK])
        sq2 = sb("sq2", [P, TOK])
        h2 = sb("h2", [P, TOK])
        out_sb = sb("out_sb", [P, TOK])
        score = sb("score", [P, SUB, EXPERTS])
        sel = sb("sel", [P, SUB, EXPERTS])
        rt = sb("rt", [P, 8, SUB * EXPERTS])
        gpair = sb("gpair", [P, 1, SUB * NG * NG])
        pair = sb("pair", [P, 2, EXPERTS, EXPERTS])
        cstack = sb("cstack", [P, TOK], BF16)
        comb = rt[:, 4].rearrange("p (s e) -> p s e", e=EXPERTS)
        crem = rt[:, 3].rearrange("p (s e) -> p s e", e=EXPERTS)
        chi = sb("chi", [P, SUB, EXPERTS], BF16)
        cmid = sb("cmid", [P, SUB, EXPERTS], BF16)
        cparts = sb("cparts", [P, SUB, ROWS])
        pick_direct = [sq2, h2]
        th = sb("th", [P, 2, TOK])
        sg = th
        cb = sb("cb", [P, 2, TOK])
        sc = sb("sc", [P, 2, TOK])
        act_o = sc

        bank = [ctx.enter_context(nc.psum_tensor(f"bank{i}", [P, TOK], F32)) for i in range(8)]
        ps_delta, ps_front, ps_du, ps_y, ps_acc, ps_g, ps_u, ps_cb = bank

        def delta_bank(g):
            return ps_g if g < LEAD and g % 2 else ps_delta

        front_pe = Steps(sem("front_pe"), FRONT_PE)
        front_act = Steps(sem("front_act"), FRONT_ACT)
        bc_act = Steps(sem("bc_act"), BC_ACT)
        front_dve = Steps(sem("front_dve"), FRONT_DVE)
        front_pool = Steps(sem("front_pool"), FRONT_POOL)
        conv = [Steps(sem(f"conv{m}"), CONV) for m in range(TILES)]
        delta_made = [Steps(sem(f"delta_made{m}"), DELTA) for m in range(TILES)]
        gate_pe = Steps(sem("gate_pe"), GATE_PE)
        gate_act = Steps(sem("gate_act"), GATE_ACT)
        gate_dve = Steps(sem("gate_dve"), GATE_DVE)
        mid_pe = Steps(sem("mid_pe"), MID_PE)
        mid_act = Steps(sem("mid_act"), MID_ACT)
        mid_dve = Steps(sem("mid_dve"), MID_DVE)
        router = sem("router")
        x_in, w_mean, w_setup, w_a, w_b, w_c = (sem(k) for k in ("x_in", "w_mean", "w_setup", "w_a", "w_b", "w_c"))
        setup_dve, setup_act, setup_pe = sem("setup_dve"), sem("setup_act"), sem("setup_pe")
        delta_in, du_in = ([sem(f"{kind}_in{tile}") for tile in range(TILES)] for kind in ("delta", "du"))
        delta_bc, du_bc, a_ready, dbu_ready = sem("delta_bc"), sem("du_bc"), sem("a_ready"), sem("dbu_ready")
        h_ready, state_saved, hc_ready, y_added = sem("h_ready"), sem("state_saved"), sem("hc_ready"), sem("y_added")
        y_read, yg_ready = sem("y_read"), sem("yg_ready")
        cb_ps, g_ps, u_ps, down = sem("cb_ps"), sem("g_ps"), sem("u_ps"), sem("down")
        cb_ready, th_ready, sg_ready, sc_ready, act_ready = sem("cb_ready"), sem("th_ready"), sem("sg_ready"), sem("sc_ready"), sem("act_ready")
        out_ready, out_done = sem("out_ready"), sem("out_done")
        SETUP_DVE = 16

        def cols(c):
            return slice(c * TOK, (c + 1) * TOK)

        def xcols(c):
            return x[:, bass_ds(c * TOK, TOK)]

        bass_ds = t["ds"]
        BIG_LOADS = [(w_gate, "w_gate"), (w_up, "w_up"), (w_down, "w_down")]
        SETUP_LOADS = [(cvec[:, 0:1], "cvec"), (A_log, "A_log"), (small, "small"), (w_mod, "w_mod")]
        FRONT_LOADS = [(w_in, "w_in"), (w_dt, "w_dt"), (w_dtp, "w_dtp"), (w_B, "w_B"), (w_C, "w_C"),
                       (pick_direct[0], "pick_direct0"), (pick_direct[1], "pick_direct1"), (pick, "pick"), (gather, "gather")]
        MID_LOADS = [(w_out, "w_out"), (w_router, "w_router"), (r_bias, "r_bias"), (ident, "ident"), (bar, "bar"),
                     (pick_e, "pick_e")]

        with nc.Block() as block:

            @block.sync
            def _(sp_eng):
                sp_eng.dma_start(x[:, 0:TOK], t["x"][:, 0:TOK]).then_inc(x_in, 16)
                sp_eng.dma_start(ones[:], t["ones"]).then_inc(w_mean, 16)
                for dst, name in SETUP_LOADS:
                    sp_eng.dma_start(dst[:], t[name]).then_inc(w_setup, 16)
                for dst, name in FRONT_LOADS:
                    sp_eng.dma_start(dst[:], t[name]).then_inc(w_a, 16)
                sp_eng.wait_ge(x_in, 16)
                sp_eng.dma_start(x[:, TOK:], t["x"][:, TOK:]).then_inc(x_in, 16)
                for dst, name in MID_LOADS:
                    sp_eng.dma_start(dst[:], t[name]).then_inc(w_b, 16)
                for dst, name in BIG_LOADS:
                    sp_eng.dma_start(dst[:], t[name]).then_inc(w_c, 16)

                def restack(n, tile):
                    ready = [(0, 0, front_act, "hi_delta"), (0, 1, front_act, "mid_delta"), (1, 0, front_act, "hi_du"),
                             (1, 1, front_act, "mid_du"), (0, 2, front_pool, "lo_delta1"), (1, 2, front_pool, "lo_du1")]
                    for kind, part, stage, step in ready:
                        read = n * GROUPS - (TILES - 1 - tile) * GROUPS // TILES
                        if kind == 0 and part == 0:
                            wait(sp_eng, delta_bc, read)
                        sp_eng.wait_ge(stage.sem, stage.done(n, step))
                        if kind == 1 and part == 0:
                            wait(sp_eng, du_bc, read)
                        for q in range(NQ):
                            sp_eng.dma_start(stack[QUAD * part:QUAD * (part + 1), kind, q, tile],
                                             parts[QUAD * q:QUAD * (q + 1), kind, part, tile]).then_inc((delta_in, du_in)[kind][tile], 16)

                def store(f):
                    sp_eng.wait_ge(out_ready, f + 2)
                    sp_eng.dma_start(t["out"][:, bass_ds(f * TOK, TOK)], out_sb[:]).then_inc(out_done, 16)

                for n in range(2):
                    for tile in range(TILES):
                        restack(n, tile)
                with sp_eng.Fori(1, CHUNKS - 1) as c:
                    for tile in range(TILES):
                        restack(c + 1, tile)
                    store(c - 1)
                store(CHUNKS - 2)
                store(CHUNKS - 1)
                sp_eng.wait_ge(out_done, 16 + 16 * CHUNKS)

            @block.tensor
            def _(pe):
                def mm(out, lhsT, rhs, start=True, stop=True):
                    return nc.tensor.matmul(out, lhsT, rhs, start=start, stop=stop)

                def front_mean(n):
                    wait(pe, gate_dve.sem, gate_dve.done(n - 1, "z1"))
                    if isinstance(n, int):
                        pe.wait_ge(x_in, 16 if n == 0 else 32)
                    mm(ps_front[:], ones[:], xcols(n)).then_inc(front_pe.sem, 1)

                def front_var(n):
                    pe.wait_ge(front_dve.sem, front_dve.done(n, "xc"))
                    pe.wait_ge(front_act.sem, front_act.done(n, "sq"))
                    mm(ps_front[:], ones[:], sq1[:]).then_inc(front_pe.sem, 1)

                def front_in(n, m):
                    if m == 0:
                        pe.wait_ge(front_dve.sem, front_dve.done(n, "h"))
                    else:
                        pe.wait_ge(front_act.sem, front_act.done(n, "xs0"))
                    mm(ps_front[:], w_in[:, m * P:(m + 1) * P], h1[:]).then_inc(front_pe.sem, 1)

                def from_u(w, bank=ps_front):
                    for m in range(TILES):
                        last = mm(bank[:], w[:, m], u[:, m], start=m == 0, stop=m == TILES - 1)
                    last.then_inc(front_pe.sem, 1)

                def front_dt(n):
                    pe.wait_ge(front_act.sem, front_act.done(n, "xs1"))
                    pe.wait_ge(front_dve.sem, front_dve.done(n, "u1"))
                    from_u(w_dt)

                def front_pre(n, m):
                    pe.wait_ge(front_act.sem, front_act.done(n, "relu0" if m else "dt"))
                    mm(ps_front[:], w_dtp[:, m * P:(m + 1) * P], dt[:]).then_inc(front_pe.sem, 1)

                def front_B(n):
                    pe.wait_ge(front_act.sem, front_act.done(n, "relu1"))
                    from_u(w_B)

                def front_C(n):
                    from_u(w_C, ps_cb)

                def gate_in(c, m):
                    if m == 0:
                        pe.wait_ge(bc_act.sem, bc_act.done(c, "B"))
                    else:
                        pe.wait_ge(gate_dve.sem, gate_dve.done(c, "z0"))
                    mm(ps_front[:], w_in[:, (TILES + m) * P:(TILES + m + 1) * P], h1[:]).then_inc(gate_pe.sem, 1)

                def mid_out(f):
                    pe.wait_ge(yg_ready, TILES * f + TILES)
                    pe.wait_ge(out_ready, f + 1)
                    for m in range(TILES):
                        last = mm(ps_acc[:], w_out[:, m], yg[:, m], start=m == 0, stop=m == TILES - 1)
                    last.then_inc(mid_pe.sem, 1)

                def mid_mean(f):
                    pe.wait_ge(mid_dve.sem, mid_dve.done(f, "x2"))
                    mm(ps_acc[:], ones[:], x2[:]).then_inc(mid_pe.sem, 1)

                def mid_var(f):
                    pe.wait_ge(mid_act.sem, mid_act.done(f, "sq"))
                    mm(ps_acc[:], ones[:], sq2[:]).then_inc(mid_pe.sem, 1)

                def mid_logits(f):
                    pe.wait_ge(mid_dve.sem, mid_dve.done(f, "h"))
                    for s in range(SUB):
                        last = mm(ps_acc[:, s * EXPERTS:(s + 1) * EXPERTS], h2[:, s * P:(s + 1) * P], w_router[:])
                    last.then_inc(mid_pe.sem, 1)

                def mid_combine(f):
                    pe.wait_ge(mid_dve.sem, mid_dve.done(f, "lo_col"))
                    for s in range(SUB):
                        last = nc.tensor.transpose(ps_acc[0:ROWS, s * P:(s + 1) * P], cparts[:, s], ident[:])
                    last.then_inc(mid_pe.sem, 1)

                def tile_of(g):
                    return g // (GROUPS // TILES), g % NQ, g // NQ % NJ

                def pick_of(g):
                    return pick_direct[g // (DIRECT // 2)][:, g % (DIRECT // 2) * P:(g % (DIRECT // 2) + 1) * P]

                def broadcast_delta(c, g):
                    tile, q, j = tile_of(g)
                    direct = isinstance(c, int) and c == 0 and g < DIRECT
                    if direct and g == 0:
                        for made in delta_made:
                            pe.wait_ge(made.sem, made.done(0, "delta"))
                    elif g % (GROUPS // TILES) == 0 or (isinstance(c, int) and c == 0 and g == DIRECT):
                        pe.wait_ge(delta_in[tile], 16 * PARTS * NQ * c + 16 * PARTS * NQ)
                    wait(pe, a_ready, c * GROUPS + (g - 1 if 0 < g < LEAD else g))
                    if direct:
                        mm(delta_bank(g)[:], pick_of(g), delta[:, tile]).then_inc(delta_bc, 1)
                        return
                    mm(delta_bank(g)[:], pick[0:ROWS, j], stack[0:ROWS, 0, q, tile]).then_inc(delta_bc, 1)

                def broadcast_du(c, g):
                    tile, q, j = tile_of(g)
                    direct = isinstance(c, int) and c == 0 and g < DIRECT
                    if direct and g == 0:
                        pe.wait_ge(front_dve.sem, front_dve.done(0, "du1"))
                    elif g % (GROUPS // TILES) == 0 or (isinstance(c, int) and c == 0 and g == DIRECT):
                        pe.wait_ge(du_in[tile], 16 * PARTS * NQ * c + 16 * PARTS * NQ)
                    wait(pe, dbu_ready, c * GROUPS + g)
                    if direct:
                        mm(ps_du[:], pick_of(g), du[:, tile]).then_inc(du_bc, 1)
                        return
                    mm(ps_du[:], pick[0:ROWS, j], stack[0:ROWS, 1, q, tile]).then_inc(du_bc, 1)

                def add_states(c, b):
                    j = b % NJ
                    pe.wait_ge(hc_ready, c * GROUPS + BLOCK * (b + 1))
                    if j == 0:
                        wait(pe, y_read, c * TILES + b // NJ)
                    for q in range(NQ):
                        last = mm(ps_y[QUAD * q:QUAD * (q + 1), :], gather[:, j], hc[:, (BLOCK * b + q) % HC_RING],
                                  start=j == 0, stop=j == NJ - 1)
                    last.then_inc(y_added, 1)

                def unit(f, k, scan):
                    if SHARED <= k < UNITS:
                        if k == SHARED:
                            pe.wait_ge(mid_dve.sem, mid_dve.done(f, "stack"))
                            if scan:
                                pe.wait_ge(bc_act.sem, bc_act.done(f + 1, "C"))
                        else:
                            pe.wait_ge(cb_ready, f * EXPERTS + k - SHARED)
                        mm(ps_cb[:], pick_e[0:ROWS, k - SHARED], cstack[0:ROWS]).then_inc(cb_ps, 1)
                    if k >= 3:
                        pe.wait_ge(act_ready, f * UNITS + k - 2)
                        mm(ps_acc[:], w_down[:, k - 3], act_o[:, (k - 3) % 2], start=k == 3,
                           stop=k == UNITS + 2).then_inc(down, 1)
                    if k < UNITS:
                        if k:
                            pe.wait_ge(sg_ready, f * UNITS + k)
                        mm(ps_g[:], w_gate[:, k], h2[:]).then_inc(g_ps, 1)
                    if 1 <= k <= UNITS:
                        if k >= 2:
                            pe.wait_ge(act_ready, f * UNITS + k - 1)
                        mm(ps_u[:], w_up[:, k - 1], h2[:]).then_inc(u_ps, 1)

                def iteration(c, scan=True, ffn=True, front=True):
                    f, n = c - 1, c + 1
                    at = SLOTS if ffn else SLOTS_NO_FFN
                    if scan:
                        broadcast_delta(c, 0)
                        broadcast_du(c, 0)
                        broadcast_delta(c, 1)
                        broadcast_du(c, 1)
                        for g in range(2, LEAD):
                            broadcast_delta(c, g)
                        if ffn:
                            front_C(c)
                    for s in range(GROUPS):
                        if scan:
                            if s + 2 < GROUPS:
                                broadcast_du(c, s + 2)
                            if s + LEAD < GROUPS:
                                broadcast_delta(c, s + LEAD)
                        if s == 0:
                            if ffn:
                                add_states(f, BLOCKS - 1)
                        if scan:
                            if s == at["PE gate_in0"]:
                                gate_in(c, 0)
                            if s == at["PE gate_in1"]:
                                gate_in(c, 1)
                        if ffn:
                            if s == 2:
                                mid_out(f)
                            if s == 4:
                                mid_mean(f)
                            if s == 6:
                                mid_var(f)
                            if s == 8:
                                mid_logits(f)
                            if s == 11:
                                mid_combine(f)
                        if front:
                            if s == at["PE mean"]:
                                front_mean(n)
                            if s == at["PE var"]:
                                front_var(n)
                            if s == at["PE in0"]:
                                front_in(n, 0)
                            if s == at["PE in1"]:
                                front_in(n, 1)
                            if s == at["PE dt"]:
                                front_dt(n)
                            if s == at["PE pre0"]:
                                front_pre(n, 0)
                            if s == at["PE pre1"]:
                                front_pre(n, 1)
                            if s == at["PE B"]:
                                front_B(n)
                        if ffn:
                            for k in units_at(s):
                                unit(f, k, scan)
                        if scan and s % BLOCK == BLOCK - 1 and s >= 2 * BLOCK - 1:
                            add_states(c, s // BLOCK - 1)

                pe.wait_ge(w_mean, 16)
                front_mean(0)
                pe.wait_ge(w_setup, 16 * len(SETUP_LOADS))
                pe.wait_ge(setup_dve, 3)
                for k in range(6):
                    last = mm(ps_acc[:, k:k + 1], w_mod[:, k // 3, (k % 3) * P:(k % 3 + 1) * P], cvec[:, 3:4])
                last.then_inc(setup_pe, 1)
                front_var(0)
                pe.wait_ge(w_a, 16 * len(FRONT_LOADS))
                front_in(0, 0)
                front_in(0, 1)
                front_dt(0)
                front_pre(0, 0)
                front_pre(0, 1)
                front_B(0)
                front_C(0)
                iteration(0, ffn=False)
                pe.wait_ge(w_b, 16 * len(MID_LOADS))
                pe.wait_ge(w_c, 16 * len(BIG_LOADS))
                with pe.Fori(1, CHUNKS - 1) as c:
                    iteration(c)
                iteration(CHUNKS - 1, front=False)
                iteration(CHUNKS, scan=False, front=False)

            @block.scalar
            def _(act):
                def ln_exp_set():
                    nc.scalar.preload_act_table_set("natural_log_exp_and_others")

                def exp_tanh_set():
                    nc.scalar.preload_act_table_set("exp_and_others")

                def front_sq(n):
                    act.wait_ge(front_dve.sem, front_dve.done(n, "xc"))
                    nc.scalar.activation(sq1[:], xc1[:], ACT.Square).then_inc(front_act.sem, 1)

                def front_rstd(n):
                    act.wait_ge(front_pe.sem, front_pe.done(n, "var"))
                    nc.scalar.activation(sq1[:], ps_front[:], ACT.Ln, bias=eps[:]).then_inc(front_act.sem, 1)
                    act.wait_ge(front_act.sem, front_act.done(n, "lnv"))
                    nc.scalar.activation(sq1[:], sq1[:], ACT.Exp, scale=-0.5).then_inc(front_act.sem, 1)

                def front_halo(n):
                    for m in range(TILES):
                        wait(act, conv[m].sem, conv[m].done(n - 1, "3"))
                    wait(act, front_act.sem, front_act.done(n - 1, "tap13"))
                    nc.scalar.copy(xs[:, :, 0:TAPS - 1], xs[:, :, TOK:]).then_inc(front_act.sem, 1)
                    act.wait_ge(front_act.sem, front_act.done(n, "halo"))

                def front_xs(n, m):
                    act.wait_ge(front_pe.sem, front_pe.done(n, f"in{m}"))
                    nc.scalar.copy(xs[:, m, TAPS - 1:], ps_front[:]).then_inc(front_act.sem, 1)
                    act.wait_ge(front_act.sem, front_act.done(n, f"xs{m}"))
                    nc.scalar.activation(cv[:, m], xs[:, m, 0:TOK], ACT.Identity, scale=conv_wh[:, m, 0:1],
                                         bias=conv_bh[:, m:m + 1]).then_inc(front_act.sem, 1)
                    wait(act, front_pool.sem, front_pool.done(n - 1, "lo_du1"))
                    if isinstance(n, int) and n == 1:
                        act.wait_ge(delta_bc, DIRECT)
                        act.wait_ge(du_bc, DIRECT)
                    for k in range(1, TAPS):
                        nc.scalar.activation(sp[:, m, k], xs[:, m, k:k + TOK], ACT.Copy,
                                             scale=conv_wh[:, m, k:k + 1]).then_inc(front_act.sem, 1)

                def front_u(n):
                    for m in range(TILES):
                        act.wait_ge(conv[m].sem, conv[m].done(n, "3"))
                        nc.scalar.activation(u[:, m], cv[:, m], ACT.Tanh).then_inc(front_act.sem, 1)

                def front_dt(n):
                    act.wait_ge(front_pe.sem, front_pe.done(n, "dt"))
                    nc.scalar.copy(dt[:], ps_front[:]).then_inc(front_act.sem, 1)

                def front_abs(n, m):
                    act.wait_ge(front_pe.sem, front_pe.done(n, f"pre{m}"))
                    nc.scalar.activation(sp[:, m, 0], ps_front[:], ACT.Abs, bias=dt_b[:, m:m + 1]).then_inc(front_act.sem, 1)
                    nc.scalar.activation(sp[:, m, 3], ps_front[:], ACT.Relu, bias=dt_b[:, m:m + 1]).then_inc(front_act.sem, 1)

                def front_exp(n, m):
                    v_exp, v_one = sp[:, m, 0], sp[:, m, 1]
                    act.wait_ge(front_act.sem, front_act.done(n, f"abs{m}"))
                    nc.scalar.activation(v_exp, v_exp, ACT.Exp, scale=-1.0).then_inc(front_act.sem, 1)
                    act.wait_ge(front_act.sem, front_act.done(n, f"exp{m}"))
                    nc.scalar.activation(v_one, v_exp, ACT.Identity, bias=1.0).then_inc(front_act.sem, 1)

                def front_ln(n):
                    for m in range(TILES):
                        nc.scalar.activation(sp[:, m, 2], sp[:, m, 0], ACT.Ln, bias=1.0).then_inc(front_act.sem, 1)

                def front_high(n, kind):
                    for arrived in (delta_in, du_in)[kind]:
                        wait(act, arrived, 16 * PARTS * NQ * n)
                    if kind == 0:
                        for made in delta_made:
                            act.wait_ge(made.sem, made.done(n, "delta"))
                    else:
                        act.wait_ge(front_dve.sem, front_dve.done(n, "du1"))
                    nc.scalar.copy(parts[:, kind, 0], (delta, du)[kind]).then_inc(front_act.sem, 1)

                def front_middle(n, kind):
                    if kind == 0:
                        act.wait_ge(front_dve.sem, front_dve.done(n, "rem_delta1"))
                    else:
                        act.wait_ge(front_pool.sem, front_pool.done(n, "rem_du1"))
                    nc.scalar.copy(parts[:, kind, 1], rem[kind]).then_inc(front_act.sem, 1)

                def front_B(n):
                    wait(act, dbu_ready, GROUPS * n)
                    act.wait_ge(front_pe.sem, front_pe.done(n, "B"))
                    nc.scalar.copy(B_bc[:], ps_front[:]).then_inc(bc_act.sem, 1)

                def front_C(n):
                    wait(act, hc_ready, GROUPS * n)
                    act.wait_ge(front_pe.sem, front_pe.done(n, "C"))
                    nc.scalar.copy(C_bc[:], ps_cb[:]).then_inc(bc_act.sem, 1)

                def gate_tanh(c, m):
                    wait(act, yg_ready, TILES * c)
                    act.wait_ge(gate_pe.sem, gate_pe.done(c, f"in{m + 2}"))
                    nc.scalar.activation(z[:, m], ps_front[:], ACT.Tanh, scale=0.5).then_inc(gate_act.sem, 1)

                def gate_skip(c):
                    wait(act, mid_pe.sem, mid_pe.done(c - 1, "out"))
                    act.wait_ge(front_dve.sem, front_dve.done(c, "u1"))
                    for m in range(TILES):
                        nc.scalar.activation(yg[:, m], u[:, m], ACT.Copy, scale=skip_D[:, m:m + 1]).then_inc(gate_act.sem, 1)

                def mid_sq(f):
                    act.wait_ge(mid_dve.sem, mid_dve.done(f, "xc"))
                    nc.scalar.activation(sq2[:], xc2[:], ACT.Square).then_inc(mid_act.sem, 1)

                def mid_rstd(f):
                    act.wait_ge(mid_pe.sem, mid_pe.done(f, "var"))
                    nc.scalar.activation(sq2[:], ps_acc[:], ACT.Ln, bias=eps[:]).then_inc(mid_act.sem, 1)
                    act.wait_ge(mid_act.sem, mid_act.done(f, "lnv"))
                    nc.scalar.activation(sq2[:], sq2[:], ACT.Exp, scale=-0.5).then_inc(mid_act.sem, 1)

                def mid_exp(f):
                    act.wait_ge(mid_pe.sem, mid_pe.done(f, "logits"))
                    nc.scalar.activation(rt[:, 0], ps_acc[:, 0:SUB * EXPERTS], ACT.Exp, scale=-1.0).then_inc(mid_act.sem, 1)

                def decay(c, g):
                    act.wait_ge(delta_bc, c * GROUPS + g + 1)
                    wait(act, h_ready, c * GROUPS + g + 1 - A_RING)
                    nc.scalar.activation(a[:, g % A_RING], delta_bank(g)[:], ACT.Exp,
                                         scale=A_neg[:, g:g + 1]).then_inc(a_ready, 1)

                def unit(f, k):
                    if k >= UNITS:
                        return
                    if k >= SHARED:
                        act.wait_ge(cb_ps, f * EXPERTS + k - SHARED + 1)
                        if k >= SHARED + 2:
                            act.wait_ge(sc_ready, f * EXPERTS + k - SHARED - 1)
                        nc.scalar.copy(cb[:, k % 2], ps_cb[:]).then_inc(cb_ready, 1)
                    act.wait_ge(g_ps, f * UNITS + k + 1)
                    if k >= 2:
                        act.wait_ge(act_ready, f * UNITS + k - 1)
                    nc.scalar.activation(th[:, k % 2], ps_g[:], ACT.Tanh, scale=0.5).then_inc(th_ready, 1)

                def iteration(c, scan=True, ffn=True, front=True):
                    f, n = c - 1, c + 1
                    at = SLOTS if ffn else SLOTS_NO_FFN
                    if scan:
                        for g in range(LEAD):
                            decay(c, g)
                    for s in range(GROUPS):
                        if scan and s + LEAD < GROUPS:
                            decay(c, s + LEAD)
                        if s == 0 and scan:
                            front_C(c)
                        if scan:
                            if s == at["ACT tanh0"]:
                                gate_tanh(c, 0)
                            if s == at["ACT tanh1"]:
                                gate_tanh(c, 1)
                            if s == at["ACT skip"]:
                                gate_skip(c)
                        if ffn:
                            if s == 5:
                                ln_exp_set()
                                mid_sq(f)
                            if s == 6:
                                mid_rstd(f)
                            if s == 8:
                                mid_exp(f)
                        if front:
                            if s == at["ACT sq"]:
                                front_sq(n)
                            if s == at["ACT rstd"]:
                                if not ffn:
                                    ln_exp_set()
                                front_rstd(n)
                                exp_tanh_set()
                            if s == at["ACT xs0"]:
                                front_halo(n)
                                front_xs(n, 0)
                            if s == at["ACT xs1"]:
                                front_xs(n, 1)
                            if s == at["ACT u"]:
                                front_u(n)
                            if s == at["ACT dt"]:
                                front_dt(n)
                            if s == at["ACT abs0"]:
                                front_abs(n, 0)
                            if s == at["ACT abs1"]:
                                front_abs(n, 1)
                                front_exp(n, 0)
                        elif s == 7 and ffn:
                            exp_tanh_set()
                        if ffn:
                            for k in units_at(s):
                                unit(f, k)
                        if front and s == at["ACT ln"]:
                            front_exp(n, 1)
                            ln_exp_set()
                            front_ln(n)
                            exp_tanh_set()
                        for kind in range(2):
                            if front and s == at["ACT high"][kind]:
                                front_high(n, kind)
                            if front and s == at["ACT middle"][kind]:
                                front_middle(n, kind)
                    if front:
                        front_B(n)

                ln_exp_set()
                act.wait_ge(w_setup, 16 * len(SETUP_LOADS))
                nc.scalar.activation(cvec[:, 1:2], cvec[:, 0:1], ACT.Exp, scale=-1.0).then_inc(setup_act, 1)
                nc.scalar.activation(A_neg[:], A_log[:], ACT.Exp).then_inc(setup_act, 1)
                act.wait_ge(setup_act, 2)
                nc.scalar.mul(A_neg[:], A_neg[:], -1.0).then_inc(setup_act, 1)
                act.wait_ge(setup_pe, 1)
                nc.scalar.copy(mod[:], ps_acc[:, 0:6]).then_inc(setup_act, 1)
                act.wait_ge(setup_act, 4)
                front_sq(0)
                act.wait_ge(setup_dve, SETUP_DVE)
                front_rstd(0)
                exp_tanh_set()
                front_halo(0)
                front_xs(0, 0)
                front_xs(0, 1)
                front_u(0)
                ln_exp_set()
                front_dt(0)
                front_abs(0, 0)
                front_abs(0, 1)
                front_exp(0, 0)
                front_exp(0, 1)
                front_ln(0)
                exp_tanh_set()
                front_B(0)
                for kind in range(2):
                    front_high(0, kind)
                for kind in range(2):
                    front_middle(0, kind)
                iteration(0, ffn=False)
                with act.Fori(1, CHUNKS - 1) as c:
                    iteration(c)
                iteration(CHUNKS - 1, front=False)
                iteration(CHUNKS, scan=False, front=False)

            @block.gpsimd
            def _(pool):
                G = nc.gpsimd

                def front_conv(n, m):
                    for k in range(1, TAPS):
                        pool.wait_ge(front_act.sem, front_act.done(n, f"tap{m}{k}"))
                        if k > 1:
                            pool.wait_ge(conv[m].sem, conv[m].done(n, str(k - 1)))
                        G.tensor_add(cv[:, m], cv[:, m], sp[:, m, k]).then_inc(conv[m].sem, 1)

                def front_delta(n, m):
                    v_exp, v_one, v_ln, v_relu = (sp[:, m, k] for k in range(4))
                    pool.wait_ge(front_dve.sem, front_dve.done(n, f"res{m}"))
                    G.tensor_sub(v_ln, v_ln, v_one).then_inc(delta_made[m].sem, 1)
                    pool.wait_ge(delta_made[m].sem, delta_made[m].done(n, "log"))
                    G.tensor_add(delta[:, m], v_ln, v_relu).then_inc(delta_made[m].sem, 1)

                def front_rem(n, m):
                    if m == 0:
                        pool.wait_ge(front_act.sem, front_act.done(n, "hi_du"))
                    G.tensor_sub(rem[1][:, m], du[:, m], parts[:, 1, 0, m]).then_inc(front_pool.sem, 1)

                def front_low(n, kind, m):
                    if m == 0:
                        pool.wait_ge(front_act.sem, front_act.done(n, ("mid_delta", "mid_du")[kind]))
                    G.tensor_sub(parts[:, kind, 2, m], rem[kind][:, m], parts[:, kind, 1, m]).then_inc(front_pool.sem, 1)

                def times_C(c, g):
                    pool.wait_ge(h_ready, c * GROUPS + g + 1)
                    wait(pool, y_added, c * BLOCKS + g // BLOCK - 1)
                    G.tensor_mul(hc[:, g % HC_RING], h[:, g % H_RING], C_bc[:]).then_inc(hc_ready, 1)

                def unit(f, k):
                    if not SHARED <= k < UNITS:
                        return
                    pool.wait_ge(sg_ready, f * UNITS + k + 1)
                    pool.wait_ge(cb_ready, f * EXPERTS + k - SHARED + 1)
                    pool.wait_ge(down, f * UNITS + k - 1)
                    G.tensor_mul(sc[:, k % 2], sg[:, k % 2], cb[:, k % 2]).then_inc(sc_ready, 1)

                def iteration(c, scan=True, ffn=True, front=True):
                    f, n = c - 1, c + 1
                    at = SLOTS if ffn else SLOTS_NO_FFN
                    if scan:
                        pool.wait_ge(bc_act.sem, bc_act.done(c, "C"))
                    for s in range(GROUPS):
                        if ffn:
                            for k in units_at(s):
                                unit(f, k)
                        if scan:
                            times_C(c, s)
                        if front:
                            for m in range(TILES):
                                if s == at["Pool conv"][m]:
                                    front_conv(n, m)
                                if s == at["Pool delta"][m]:
                                    front_delta(n, m)
                                if s == at["Pool rem_du"][m]:
                                    front_rem(n, m)
                                if s == at["Pool lo_delta"][m]:
                                    front_low(n, 0, m)
                                if s == at["Pool lo_du"][m]:
                                    front_low(n, 1, m)

                front_conv(0, 0)
                front_delta(0, 0)
                for m in range(TILES):
                    front_rem(0, m)
                for kind in range(2):
                    for m in range(TILES):
                        front_low(0, kind, m)
                iteration(0, ffn=False)
                with pool.Fori(1, CHUNKS - 1) as c:
                    iteration(c)
                iteration(CHUNKS - 1, front=False)
                iteration(CHUNKS, scan=False, front=False)

            @block.vector
            def _(dve):
                V = nc.vector
                one_ca, one_cb, ga_half, gb = (scale1[:, k:k + 1] for k in range(4))
                sa, sb_ = mod[:, 0:1], mod[:, 3:4]

                def setup():
                    n = [0]

                    def link(ins):
                        n[0] += 1
                        ins.then_inc(setup_dve, 1)
                        dve.wait_ge(setup_dve, n[0])

                    dve.wait_ge(setup_act, 1)
                    link(V.tensor_scalar(cvec[:, 2:3], cvec[:, 1:2], 1.0, None, ALU.add))
                    link(V.reciprocal(cvec[:, 1:2], cvec[:, 2:3]))
                    link(V.tensor_mul(cvec[:, 3:4], cvec[:, 0:1], cvec[:, 1:2]))
                    V.memset(eps[:], EPS)
                    V.memset(xs[:], 0.0)
                    V.memset(cparts[:], 0.0)
                    link(V.memset(state[:], 0.0))
                    link(V.tensor_scalar(conv_wh[:], conv_w, 0.5, None, ALU.mult))
                    link(V.tensor_scalar(conv_bh[:], conv_b, 0.5, None, ALU.mult))
                    front_xc(0)
                    dve.wait_ge(setup_act, 4)
                    link(V.tensor_scalar(one_ca, mod[:, 1:2], 1.0, None, ALU.add))
                    link(V.tensor_scalar(one_cb, mod[:, 4:5], 1.0, None, ALU.add))
                    for dst, k, sign in ((ga_half, 2, 1.0), (gb, 5, 2.0)):
                        link(V.tensor_scalar(scale1[:, 4:5], mod[:, k:k + 1], 0.0, sign, ALU.is_ge, ALU.mult))
                        link(V.scalar_tensor_tensor(scale1[:, 7:8], mod[:, k:k + 1], -1.0, mod[:, k:k + 1], ALU.mult, ALU.max))
                        V.tensor_scalar(scale1[:, 5:6], scale1[:, 7:8], 0.25, None, ALU.max)
                        link(V.tensor_scalar(scale1[:, 6:7], scale1[:, 4:5], sign / 2, None, ALU.subtract))
                        if k == 2:
                            link(V.tensor_mul(dst, scale1[:, 6:7], scale1[:, 5:6]))
                        else:
                            V.tensor_mul(dst, scale1[:, 6:7], scale1[:, 5:6]).then_inc(setup_dve, 1)
                    assert n[0] == SETUP_DVE - 1, n
                    dve.wait_ge(setup_dve, SETUP_DVE)
                    dve.sem_inc(out_ready, 1)
                    dve.sem_inc(out_done, 16)

                def f_wait(n, step):
                    dve.wait_ge(front_dve.sem, front_dve.done(n, step))

                def front_xc(n):
                    dve.wait_ge(front_pe.sem, front_pe.done(n, "mean"))
                    V.tensor_sub(xc1[:], xcols(n), ps_front[:]).then_inc(front_dve.sem, 1)

                def front_h(n):
                    dve.wait_ge(front_act.sem, front_act.done(n, "rstd"))
                    V.tensor_mul(xc1[:], xc1[:], sq1[:]).then_inc(front_dve.sem, 1)
                    f_wait(n, "xn")
                    V.tensor_scalar(h1[:], xc1[:], one_ca, sa, ALU.mult, ALU.add).then_inc(front_dve.sem, 1)

                def front_u(n):
                    for m in range(TILES):
                        dve.wait_ge(front_act.sem, front_act.done(n, f"ut{m}"))
                        V.scalar_tensor_tensor(u[:, m], u[:, m], 1.0, cv[:, m], ALU.add, ALU.mult).then_inc(front_dve.sem, 1)

                def front_res(n):
                    for m in range(TILES):
                        v_exp, v_one = sp[:, m, 0], sp[:, m, 1]
                        dve.wait_ge(front_act.sem, front_act.done(n, f"ln{m}"))
                        V.scalar_tensor_tensor(v_one, v_one, 1.0, v_exp, ALU.subtract, ALU.subtract).then_inc(front_dve.sem, 1)

                def first_conv(m):
                    for k in range(1, TAPS):
                        dve.wait_ge(front_act.sem, front_act.done(0, f"tap{m}{k}"))
                        if k > 1:
                            dve.wait_ge(conv[m].sem, conv[m].done(0, str(k - 1)))
                        V.tensor_add(cv[:, m], cv[:, m], sp[:, m, k]).then_inc(conv[m].sem, 1)

                def first_delta(m):
                    v_exp, v_one, v_ln, v_relu = (sp[:, m, k] for k in range(4))
                    f_wait(0, f"res{m}")
                    V.tensor_sub(v_ln, v_ln, v_one).then_inc(delta_made[m].sem, 1)
                    dve.wait_ge(delta_made[m].sem, delta_made[m].done(0, "log"))
                    V.tensor_add(delta[:, m], v_ln, v_relu).then_inc(delta_made[m].sem, 1)

                def front_du(n):
                    for m in range(TILES):
                        dve.wait_ge(delta_made[m].sem, delta_made[m].done(n, "delta"))
                        V.tensor_mul(du[:, m], delta[:, m], u[:, m]).then_inc(front_dve.sem, 1)

                def front_rem(n):
                    dve.wait_ge(front_act.sem, front_act.done(n, "hi_delta"))
                    for m in range(TILES):
                        V.tensor_sub(rem[0][:, m], delta[:, m], parts[:, 0, 0, m]).then_inc(front_dve.sem, 1)

                def gate_z(c, m):
                    dve.wait_ge(gate_act.sem, gate_act.done(c, f"tanh{m}"))
                    V.scalar_tensor_tensor(z[:, m], z[:, m], 1.0, ps_front[:], ALU.add, ALU.mult).then_inc(gate_dve.sem, 1)

                def gate(c, m):
                    dve.wait_ge(y_added, c * BLOCKS + (m + 1) * NJ)
                    dve.wait_ge(gate_act.sem, gate_act.done(c, f"skip{m}"))
                    V.tensor_add(yg[:, m], yg[:, m], ps_y[:]).then_inc(y_read, 1)
                    dve.wait_ge(y_read, c * TILES + m + 1)
                    V.tensor_mul(yg[:, m], yg[:, m], z[:, m]).then_inc(yg_ready, 1)

                def m_wait(f, step):
                    dve.wait_ge(mid_dve.sem, mid_dve.done(f, step))

                def mid_x2(f):
                    dve.wait_ge(mid_pe.sem, mid_pe.done(f, "out"))
                    V.scalar_tensor_tensor(x2[:], ps_acc[:], ga_half, xcols(f), ALU.mult, ALU.add).then_inc(mid_dve.sem, 1)

                def mid_xc(f):
                    dve.wait_ge(mid_pe.sem, mid_pe.done(f, "mean"))
                    m_wait(f, "x2")
                    V.tensor_sub(xc2[:], x2[:], ps_acc[:]).then_inc(mid_dve.sem, 1)

                def mid_h(f):
                    dve.wait_ge(mid_act.sem, mid_act.done(f, "rstd"))
                    V.tensor_mul(xc2[:], xc2[:], sq2[:]).then_inc(mid_dve.sem, 1)
                    m_wait(f, "xn")
                    V.tensor_scalar(h2[:], xc2[:], one_cb, sb_, ALU.mult, ALU.add).then_inc(mid_dve.sem, 1)

                class Router:

                    def __init__(self, f, first):
                        self.f, self.n = f, first

                    def step(self, ins):
                        self.n += 1
                        ins.then_inc(router, 1)

                    def settle(self, back=0):
                        dve.wait_ge(router, self.f * ROUTER_STEPS + (self.n - back))

                    def link(self, ins):
                        self.step(ins)
                        self.settle()

                def by_expert(k):
                    return rt[:, k].rearrange("p (s e) -> p s e", e=EXPERTS)

                SG = SUB * NG
                den, biased, masked, rank = (by_expert(k) for k in range(4))

                def route_groups(f):
                    r = Router(f, 0)
                    link, step = r.link, r.step
                    dve.wait_ge(mid_act.sem, mid_act.done(f, "explog"))
                    link(V.tensor_scalar(den, den, 1.0, None, ALU.add))
                    link(V.reciprocal(score[:], den))
                    link(V.tensor_tensor(biased, score[:], r_bias[:, :].unsqueeze(1).broadcast_to([P, SUB, EXPERTS]), ALU.add))
                    four = rt[:, 1].rearrange("p (g b a) -> p g b a", a=2, b=2)
                    hi2 = rt[:, 5, 0:2 * SG].rearrange("p (g b) -> p g b", b=2)
                    lo2 = rt[:, 6, 0:2 * SG].rearrange("p (g b) -> p g b", b=2)
                    top1, mid1, low1, gs = (rt[:, 7, k * SG:(k + 1) * SG] for k in range(4))
                    step(V.tensor_tensor(hi2, four[:, :, :, 0], four[:, :, :, 1], ALU.max))
                    link(V.tensor_tensor(lo2, four[:, :, :, 0], four[:, :, :, 1], ALU.min))
                    step(V.tensor_tensor(top1, hi2[:, :, 0], hi2[:, :, 1], ALU.max))
                    step(V.tensor_tensor(mid1, hi2[:, :, 0], hi2[:, :, 1], ALU.min))
                    link(V.tensor_tensor(low1, lo2[:, :, 0], lo2[:, :, 1], ALU.max))
                    link(V.tensor_tensor(mid1, mid1, low1, ALU.max))
                    link(V.tensor_tensor(gs, top1, mid1, ALU.add))
                    gs3 = gs.rearrange("p (s g) -> p s g", g=NG)
                    gj = gs3.unsqueeze(2).broadcast_to([P, SUB, NG, NG])
                    gi = gs3.unsqueeze(3).broadcast_to([P, SUB, NG, NG])
                    diff = gpair[:, 0].rearrange("p (s i j) -> p s i j", i=NG, j=NG)
                    link(V.tensor_tensor(diff, gj, gi, ALU.subtract))
                    link(V.tensor_tensor(diff, diff, bar[:, 0:NG, 0:NG].unsqueeze(1).broadcast_to([P, SUB, NG, NG]), ALU.is_gt))
                    grank, gm1 = rt[:, 5, 0:SG], rt[:, 6, 0:SG]
                    link(V.tensor_reduce(grank, gpair[:, 0].rearrange("p (q j) -> p q j", j=NG), AX.X, ALU.add))
                    link(V.tensor_scalar(grank, grank, float(TOPG), None, ALU.is_lt))
                    s4 = rt[:, 1].rearrange("p (q e) -> p q e", e=EPG)
                    m4 = rt[:, 2].rearrange("p (q e) -> p q e", e=EPG)
                    step(V.tensor_tensor(m4, s4, grank.unsqueeze(2).broadcast_to([P, SG, EPG]), ALU.mult))
                    link(V.tensor_scalar(gm1, grank, 1.0, None, ALU.subtract))
                    step(V.tensor_tensor(m4, m4, gm1.unsqueeze(2).broadcast_to([P, SG, EPG]), ALU.add))
                    assert r.n == ROUTER_FIRST, r.n

                def route_ranks(f, first):
                    r = Router(f, ROUTER_FIRST + 3 * first)
                    r.settle()
                    for s in (0, 1):
                        ej = masked[:, first + s].unsqueeze(1).broadcast_to([P, EXPERTS, EXPERTS])
                        ei = masked[:, first + s].unsqueeze(2).broadcast_to([P, EXPERTS, EXPERTS])
                        r.step(V.tensor_tensor(pair[:, s], ej, ei, ALU.subtract))
                    for s in (0, 1):
                        r.settle(1)
                        r.step(V.tensor_tensor(pair[:, s], pair[:, s], bar[:], ALU.is_gt))
                    for s in (0, 1):
                        r.settle(1)
                        r.step(V.tensor_reduce(rank[:, first + s], pair[:, s], AX.X, ALU.add))

                def route_weights(f):
                    r = Router(f, ROUTER_FIRST + 3 * SUB)
                    link = r.link
                    r.settle()
                    link(V.tensor_scalar(sel[:], rank, float(TOPK), None, ALU.is_lt))
                    link(V.tensor_tensor(sel[:], sel[:], score[:], ALU.mult))
                    total, inverse = rt[:, 6, 0:SUB], rt[:, 5, 0:SUB]
                    link(V.tensor_reduce(total, sel[:], AX.X, ALU.add))
                    link(V.tensor_scalar(total, total, 1e-20, None, ALU.add))
                    link(V.reciprocal(inverse, total))
                    assert r.n == ROUTER_STEPS, r.n
                    V.scalar_tensor_tensor(comb, sel[:], ROUTE_SCALE / 2,
                                           inverse.unsqueeze(2).broadcast_to([P, SUB, EXPERTS]),
                                           ALU.mult, ALU.mult).then_inc(mid_dve.sem, 1)

                def mid_parts(f):
                    def column(k):
                        return cparts[:, :, QUAD * k:QUAD * k + EXPERTS]

                    m_wait(f, "combine")
                    V.tensor_copy(chi[:], comb).then_inc(mid_dve.sem, 1)
                    m_wait(f, "hi")
                    V.tensor_sub(crem, comb, chi[:]).then_inc(mid_dve.sem, 1)
                    m_wait(f, "rem")
                    V.tensor_copy(cmid[:], crem).then_inc(mid_dve.sem, 1)
                    V.tensor_copy(column(0), chi[:]).then_inc(mid_dve.sem, 1)
                    m_wait(f, "mid")
                    V.tensor_copy(column(1), cmid[:]).then_inc(mid_dve.sem, 1)
                    V.tensor_sub(column(2), crem, cmid[:]).then_inc(mid_dve.sem, 1)

                def mid_stack(f):
                    dve.wait_ge(mid_pe.sem, mid_pe.done(f, "combineT"))
                    V.tensor_copy(cstack[0:ROWS], ps_acc[0:ROWS]).then_inc(mid_dve.sem, 1)

                def times_B(c, g):
                    dve.wait_ge(du_bc, c * GROUPS + g + 1)
                    if g == 0:
                        dve.wait_ge(bc_act.sem, bc_act.done(c, "B"))
                    wait(dve, h_ready, c * GROUPS + g - 1)
                    V.tensor_mul(dbu[:, g % 2], B_bc[:], ps_du[:]).then_inc(dbu_ready, 1)

                def scan_group(c, g):
                    dve.wait_ge(a_ready, c * GROUPS + g + 1)
                    dve.wait_ge(dbu_ready, c * GROUPS + g + 1)
                    wait(dve, hc_ready, c * GROUPS + g + 1 - H_RING)
                    wait(dve, state_saved, c * BLOCKS + g // BLOCK - 1)
                    V.tensor_tensor_scan(h[:, g % H_RING], a[:, g % A_RING], dbu[:, g % 2], state[:, g:g + 1],
                                         ALU.mult, ALU.add).then_inc(h_ready, 1)
                    if g % BLOCK == BLOCK - 1:
                        dve.wait_ge(h_ready, c * GROUPS + g + 1)
                        at = (g + 1 - BLOCK) % H_RING
                        V.tensor_copy(state[:, g + 1 - BLOCK:g + 1], h[:, at:at + BLOCK, TOK - 1]).then_inc(state_saved, 1)

                def unit(f, k):
                    if k < UNITS:
                        dve.wait_ge(th_ready, f * UNITS + k + 1)
                        V.scalar_tensor_tensor(sg[:, k % 2], th[:, k % 2], 1.0, ps_g[:], ALU.add, ALU.mult).then_inc(sg_ready, 1)
                    if 1 <= k <= UNITS:
                        e = k - 1
                        dve.wait_ge(u_ps, f * UNITS + e + 1)
                        if e >= 2:
                            dve.wait_ge(down, f * UNITS + e - 1)
                        if e >= SHARED:
                            dve.wait_ge(sc_ready, f * EXPERTS + e - SHARED + 1)
                            V.tensor_mul(act_o[:, e % 2], sc[:, e % 2], ps_u[:]).then_inc(act_ready, 1)
                        else:
                            dve.wait_ge(sg_ready, f * UNITS + e + 1)
                            V.scalar_tensor_tensor(act_o[:, e % 2], sg[:, e % 2], 0.5, ps_u[:], ALU.mult, ALU.mult).then_inc(act_ready, 1)

                def finish(f):
                    dve.wait_ge(down, (f + 1) * UNITS)
                    dve.wait_ge(out_done, 16 * f + 16)
                    V.scalar_tensor_tensor(out_sb[:], ps_acc[:], gb, x2[:], ALU.mult, ALU.add).then_inc(out_ready, 1)

                def iteration(c, scan=True, ffn=True, front=True):
                    f, n = c - 1, c + 1
                    at = SLOTS if ffn else SLOTS_NO_FFN
                    if scan:
                        times_B(c, 0)
                    for s in range(GROUPS):
                        if scan:
                            if s + 1 < GROUPS:
                                times_B(c, s + 1)
                            scan_group(c, s)
                        if scan:
                            if s == at["DVE z0"]:
                                gate_z(c, 0)
                            if s == at["DVE z1"]:
                                gate_z(c, 1)
                            if s == 21:
                                gate(c, 0)
                        if ffn:
                            if s == 1:
                                gate(f, 1)
                            if s == 3:
                                mid_x2(f)
                            if s == 5:
                                mid_xc(f)
                            if s == 7:
                                mid_h(f)
                            if s == 9:
                                route_groups(f)
                            if s == 10:
                                route_ranks(f, 0)
                                route_ranks(f, 2)
                            if s == 11:
                                route_weights(f)
                                mid_parts(f)
                            for k in units_at(s - 1):
                                unit(f, k)
                            if s == 11:
                                mid_stack(f)
                        if front:
                            if s == at["DVE xc"]:
                                front_xc(n)
                            if s == at["DVE h"]:
                                front_h(n)
                            if s == at["DVE u"]:
                                front_u(n)
                            if s == at["DVE res"]:
                                front_res(n)
                            if s == at["DVE du"]:
                                front_du(n)
                            if s == at["DVE rem"]:
                                front_rem(n)
                    if ffn:
                        finish(f)

                setup()
                front_h(0)
                first_conv(1)
                front_u(0)
                front_res(0)
                first_delta(1)
                front_du(0)
                front_rem(0)
                iteration(0, ffn=False)
                with dve.Fori(1, CHUNKS - 1) as c:
                    iteration(c)
                iteration(CHUNKS - 1, front=False)
                iteration(CHUNKS, scan=False, front=False)


def units_at(s):
    return [k for k, at in enumerate(UNIT_SLOTS) if at == s]


def program(nc, args):
    from contextlib import ExitStack

    import concourse.bass as bass
    from concourse import mybir

    build(nc, mybir, ExitStack, {**args, "ds": bass.ds})


def kernel(**inputs):
    import ml_dtypes
    import numpy as np
    import concourse.bacc as bacc
    from concourse import mybir
    from concourse.bass_utils import run_bass_kernel_spmd

    w = {k.replace("L0_", ""): np.asarray(v) for k, v in inputs.items()}

    def tiles(m):
        return m.reshape(-1, P, m.shape[-1]).transpose(1, 0, 2)

    part = np.arange(P)
    f32 = np.float32
    xp = w["attn_x_proj_w"]
    pad = np.zeros((P, DI), f32)
    pad[:RANK] = xp[:RANK]
    dtp = np.zeros((P, DI), f32)
    dtp[:RANK] = w["attn_dt_proj_w"].T
    g = np.arange(GROUPS)
    first = P * (g // (GROUPS // TILES)) + QUAD * (g % NQ) + CH * (g // NQ % NJ)
    A_log = w["attn_A_log"][first[None, :] + (part % CH)[:, None], (part // CH)[:, None]]
    pick = np.zeros((P, NJ, P), f32)
    gather = np.zeros((P, NJ, QUAD), f32)
    for j in range(NJ):
        for k in range(PARTS):
            pick[QUAD * k + CH * j + part % CH, j, part] = 1
        gather[part, j, CH * j + part % CH] = 1
    direct = np.zeros((P, DIRECT, P), f32)
    for k in range(DIRECT):
        direct[first[k] + part % CH, k, part] = 1
    pick_e = np.zeros((P, EXPERTS, P), f32)
    for e in range(EXPERTS):
        for k in range(PARTS):
            pick_e[QUAD * k + e, e] = 1
    i = np.arange(EXPERTS)
    bar = np.broadcast_to(np.where(i[None, :] < i[:, None], -np.finfo(f32).tiny, 0).astype(f32), (P, EXPERTS, EXPERTS))

    def units(shared, experts):
        return np.concatenate([shared, experts], axis=1)

    halves = lambda m: m.reshape(P, SHARED, P)
    small = np.concatenate([tiles(w["attn_conv_w"][:, 0]).reshape(P, -1)] +
                           [tiles(w[k][:, None]).reshape(P, -1) for k in ("attn_conv_b", "attn_dt_proj_b", "attn_D")], axis=1)
    arrays = {
        "x": w["attn_x"][0].T,
        "w_in": w["attn_in_proj_w"].T,
        "w_dt": tiles(pad.T),
        "w_B": tiles(xp[RANK + part // CH].T),
        "w_C": tiles(xp[RANK + NS + part // CH].T),
        "w_dtp": dtp,
        "w_out": tiles(w["attn_out_proj_w"].T),
        "small": small,
        "A_log": A_log,
        "w_router": w["ffn_router_w"].T,
        "r_bias": np.broadcast_to(w["ffn_bias"], (P, EXPERTS)),
        "w_gate": units(halves(w["ffn_sh_gate_w"]), w["ffn_gate_w"].transpose(1, 0, 2)),
        "w_up": units(halves(w["ffn_sh_up_w"]), w["ffn_up_w"].transpose(1, 0, 2)),
        "w_down": units(w["ffn_sh_down_w"].reshape(SHARED, P, DM).transpose(1, 0, 2), w["ffn_down_w"].transpose(1, 0, 2)),
        "ones": np.full((P, P), 1.0 / DM, f32),
        "ident": np.eye(P, dtype=f32),
        "bar": bar,
        "pick": pick.astype(ml_dtypes.bfloat16),
        "gather": gather,
        "pick_direct0": direct[:, :DIRECT // 2].reshape(P, -1),
        "pick_direct1": direct[:, DIRECT // 2:].reshape(P, -1),
        "pick_e": pick_e.astype(ml_dtypes.bfloat16),
        "w_mod": w["wmod"].reshape(P, 2, 3 * P),
        "cvec": w["c"].reshape(P, 1),
    }
    nc = bacc.Bacc("TRN2", target_bir_lowering=False, num_devices=1)
    feed, args = {}, {}
    for name, a in arrays.items():
        a = np.ascontiguousarray(a)
        feed[f"in_{name}"] = a
        args[name] = nc.dram_tensor(f"in_{name}", a.shape, mybir.dt.from_np(a.dtype), kind="ExternalInput").ap()
    args["out"] = nc.dram_tensor("out_T", (DM, SEQ), mybir.dt.float32, kind="ExternalOutput").ap()
    program(nc, args)
    r = run_bass_kernel_spmd(nc, [feed], core_ids=[0])
    return np.ascontiguousarray(r.results[0]["out_T"].T)[None]
```
